# Optimizing a Trainium2 kernel written in Bass

```python
import numpy as np
import jax
import jax.numpy as jnp

def _softmax(x, axis=-1):
    return jax.nn.softmax(x, axis=axis)

def _gelu(x):
    return jax.nn.gelu(x, approximate=True)

def _silu(x):
    return jax.nn.silu(x)

def _sigmoid(x):
    return jax.nn.sigmoid(x)

def _layernorm(x, axis=-1, eps=1e-05):
    m = jnp.mean(x, axis=axis, keepdims=True)
    v = jnp.var(x, axis=axis, keepdims=True)
    return (x - m) / jnp.sqrt(v + eps)

def _scatter_add(tgt, idx, src, axis=0):
    return tgt.at[idx].add(src)

def _segment_sum(src, seg, n):
    return jax.ops.segment_sum(src, seg, n)
kernel_name = 'mk_flamingo_gated_d2_seqx_r8_68eb39'

def setup_inputs(seed: int=0):
    np.random.seed(seed)
    _w = jnp.asarray

    def _rec_inputs():
        import jax
        import jax.numpy as jnp
        _rk = jax.random.key(seed)
        x = -0.0002928 + 1 * jax.random.normal(jax.random.fold_in(_rk, 1), (16, 256, 128), jnp.float32)
        _lenS = 256 - jax.random.randint(jax.random.fold_in(_rk, 7), (16,), 0, max(1, 256 // 4) + 1, jnp.int32)
        _lenS2 = 1601 - jax.random.randint(jax.random.fold_in(_rk, 8), (16,), 0, max(1, 1601 // 4) + 1, jnp.int32)
        _ctx_1024P = jax.random.normal(jax.random.fold_in(_rk, 11), (16, 16, 128), jnp.float32)
        _ctx_1024c = jax.random.dirichlet(jax.random.fold_in(_rk, 511), 0.3 * jnp.ones((16,), jnp.float32), (16, 1601))
        _ctx_1024t = jnp.einsum('bsk,bkd->bsd', _ctx_1024c, _ctx_1024P)
        _ctx_1024t = _ctx_1024t * jax.lax.rsqrt(jnp.mean(jnp.square(_ctx_1024t)) + 1e-12) * 0.953939
        ctx_1024 = -1.39393e-06 + 0.999914 * (_ctx_1024t + 0.3 * jax.random.normal(jax.random.fold_in(_rk, 611), (16, 1601, 128), jnp.float32))
        _validS = jnp.arange(256)[None, :] < _lenS[:, None]
        _validS2 = jnp.arange(1601)[None, :] < _lenS2[:, None]
        _causal = jnp.tril(jnp.ones((256, 256), dtype=bool))
        mask_BxS2_bf1 = jnp.ones((16, 1601), dtype=bool)
        mask_Bx1xSxS2_ik1 = jnp.where(jnp.broadcast_to(_validS2[:, None, None, :], (16, 1, 256, 1601)), 1, 0).astype(jnp.int32)
        _g = jax.random.normal(jax.random.fold_in(_rk, 9001), (2, 2), jnp.float32)
        _g = jnp.sign(_g) * jnp.maximum(jnp.abs(_g), 1.0) + (_g == 0) * 1.0
        g_xattn = _g[0]
        g_ffn = _g[1]
        return (x, ctx_1024, mask_BxS2_bf1, mask_Bx1xSxS2_ik1, g_xattn, g_ffn)
    x, ctx_1024, mask_BxS2_bf1, mask_Bx1xSxS2_ik1, g_xattn, g_ffn = _rec_inputs()

    def _L0_xattn_setup():
        import jax, jax.numpy as jnp
        import numpy as np
        N_HEADS = 16
        D_MODEL = 128
        HEAD_DIM = D_MODEL // N_HEADS
        MASK_FILL = -100000000.0

        def _split_heads(x):
            B, S, _ = x.shape
            return x.reshape(B, S, N_HEADS, HEAD_DIM).transpose(0, 2, 1, 3)
        key = jax.random.key(seed)
        ks = jax.random.split(key, 12)
        B, L, P = (2, 256, 256)
        s = 1.0 / np.sqrt(D_MODEL).astype(np.float32)
        inp = {'q': jax.random.normal(ks[0], (B, L, D_MODEL), dtype=jnp.float32), 'k': jax.random.normal(ks[1], (B, P, D_MODEL), dtype=jnp.float32), 'v': jax.random.normal(ks[2], (B, P, D_MODEL), dtype=jnp.float32), 'attention_mask': jnp.ones((B, P), dtype=bool), 'Wq': jax.random.normal(ks[3], (D_MODEL, D_MODEL), dtype=jnp.float32) * s, 'bq': jnp.zeros((D_MODEL,), dtype=jnp.float32), 'Wk': jax.random.normal(ks[4], (D_MODEL, D_MODEL), dtype=jnp.float32) * s, 'bk': jnp.zeros((D_MODEL,), dtype=jnp.float32), 'Wv': jax.random.normal(ks[5], (D_MODEL, D_MODEL), dtype=jnp.float32) * s, 'bv': jnp.zeros((D_MODEL,), dtype=jnp.float32), 'Wo': jax.random.normal(ks[6], (D_MODEL, D_MODEL), dtype=jnp.float32) * s, 'bo': jnp.zeros((D_MODEL,), dtype=jnp.float32)}
        return inp
    _L0_xattn_all = _L0_xattn_setup()
    _L0_xattn_in = {k: v for k, v in _L0_xattn_all.items() if k in ('Wq', 'bq', 'Wk', 'bk', 'Wv', 'bv', 'Wo', 'bo')}
    del _L0_xattn_all

    def _L0_ffn_setup():
        import jax, jax.numpy as jnp
        import numpy as np
        EPS = 1e-06
        LN_EPS = 1e-05

        def _absmean_core(W):
            gamma = jnp.mean(jnp.abs(W)) + EPS
            Ws = W / gamma
            Wq = jnp.sign(Ws) * jnp.minimum(jnp.round(jnp.abs(Ws)), 1.0)
            return (Wq, gamma)

        @jax.custom_vjp
        def absmean(W):
            return _absmean_core(W)[0]

        def _absmean_fwd(W):
            Wq, gamma = _absmean_core(W)
            return (Wq, gamma)

        def _absmean_bwd(gamma, g):
            return (g / gamma,)
        absmean.defvjp(_absmean_fwd, _absmean_bwd)

        def layernorm(x, w, b, eps=LN_EPS):
            mu = jnp.mean(x, axis=-1, keepdims=True)
            var = jnp.mean((x - mu) ** 2, axis=-1, keepdims=True)
            return (x - mu) * jax.lax.rsqrt(var + eps) * w + b
        key = jax.random.key(seed)
        k1, k2, k3 = jax.random.split(key, 3)
        d, h = (128, 512)
        B, T = (8, 256)
        return {'x': jax.random.normal(k1, (B, T, d), jnp.float32), 'W_fc': jax.random.normal(k2, (h, d), jnp.float32), 'ln_w': jnp.ones((h,), jnp.float32), 'ln_b': jnp.zeros((h,), jnp.float32), 'W_proj': jax.random.normal(k3, (d, h), jnp.float32)}
    _L0_ffn_all = _L0_ffn_setup()
    _L0_ffn_in = {k: v for k, v in _L0_ffn_all.items() if k in ('W_fc', 'ln_w', 'ln_b', 'W_proj')}
    del _L0_ffn_all

    def _L1_xattn_setup():
        import jax, jax.numpy as jnp
        import numpy as np
        D_MODEL = 128
        HEADS = 16
        D_K = D_MODEL // HEADS
        NEG_INF = -10000000000.0
        key = jax.random.key(seed)
        ks = jax.random.split(key, 10)
        n, s = (2, 256)
        inp = {'value': jax.random.normal(ks[0], (n, s, D_MODEL), dtype=jnp.float32), 'key': jax.random.normal(ks[1], (n, s, D_MODEL), dtype=jnp.float32), 'query': jax.random.normal(ks[2], (n, s, D_MODEL), dtype=jnp.float32), 'mask': jax.random.randint(ks[3], (n, 1, s, s), 0, 2, dtype=jnp.int32), 'Wq': jax.random.normal(ks[4], (D_MODEL, D_MODEL), dtype=jnp.float32) * D_MODEL ** (-0.5), 'Wk': jax.random.normal(ks[5], (D_MODEL, D_MODEL), dtype=jnp.float32) * D_MODEL ** (-0.5), 'Wv': jax.random.normal(ks[6], (D_MODEL, D_MODEL), dtype=jnp.float32) * D_MODEL ** (-0.5), 'Wo': jax.random.normal(ks[7], (D_MODEL, D_MODEL), dtype=jnp.float32) * D_MODEL ** (-0.5), 'bo': jax.random.normal(ks[8], (D_MODEL,), dtype=jnp.float32) * 0.01}
        return inp
    _L1_xattn_all = _L1_xattn_setup()
    _L1_xattn_in = {k: v for k, v in _L1_xattn_all.items() if k in ('Wq', 'Wk', 'Wv', 'Wo', 'bo')}
    del _L1_xattn_all

    def _L1_ffn_setup():
        import jax, jax.numpy as jnp
        import numpy as np
        B, S, H, F, E, K = (2, 128, 128, 256, 8, 2)
        key = jax.random.key(seed)
        ks = jax.random.split(key, 5)
        scale_h = 1.0 / np.sqrt(H)
        scale_f = 1.0 / np.sqrt(F)
        return {'inputs': jax.random.normal(ks[0], (B, S, H), dtype=jnp.float32), 'router_w': jax.random.normal(ks[1], (H, E), dtype=jnp.float32) * scale_h, 'w1': jax.random.normal(ks[2], (E, H, F), dtype=jnp.float32) * scale_h, 'w3': jax.random.normal(ks[3], (E, H, F), dtype=jnp.float32) * scale_h, 'w2': jax.random.normal(ks[4], (E, F, H), dtype=jnp.float32) * scale_f}
    _L1_ffn_all = _L1_ffn_setup()
    _L1_ffn_in = {k: v for k, v in _L1_ffn_all.items() if k in ('router_w', 'w1', 'w3', 'w2')}
    del _L1_ffn_all
    return {'x': x, 'ctx_1024': ctx_1024, 'mask_BxS2_bf1': mask_BxS2_bf1, 'mask_Bx1xSxS2_ik1': mask_Bx1xSxS2_ik1, 'g_xattn': g_xattn, 'g_ffn': g_ffn, 'L0_xattn_Wq': _L0_xattn_in['Wq'], 'L0_xattn_bq': _L0_xattn_in['bq'], 'L0_xattn_Wk': _L0_xattn_in['Wk'], 'L0_xattn_bk': _L0_xattn_in['bk'], 'L0_xattn_Wv': _L0_xattn_in['Wv'], 'L0_xattn_bv': _L0_xattn_in['bv'], 'L0_xattn_Wo': _L0_xattn_in['Wo'], 'L0_xattn_bo': _L0_xattn_in['bo'], 'L0_ffn_W_fc': _L0_ffn_in['W_fc'], 'L0_ffn_ln_w': _L0_ffn_in['ln_w'], 'L0_ffn_ln_b': _L0_ffn_in['ln_b'], 'L0_ffn_W_proj': _L0_ffn_in['W_proj'], 'L1_xattn_Wq': _L1_xattn_in['Wq'], 'L1_xattn_Wk': _L1_xattn_in['Wk'], 'L1_xattn_Wv': _L1_xattn_in['Wv'], 'L1_xattn_Wo': _L1_xattn_in['Wo'], 'L1_xattn_bo': _L1_xattn_in['bo'], 'L1_ffn_router_w': _L1_ffn_in['router_w'], 'L1_ffn_w1': _L1_ffn_in['w1'], 'L1_ffn_w3': _L1_ffn_in['w3'], 'L1_ffn_w2': _L1_ffn_in['w2']}

def reference(x, ctx_1024, mask_BxS2_bf1, mask_Bx1xSxS2_ik1, g_xattn, g_ffn, L0_xattn_Wq, L0_xattn_bq, L0_xattn_Wk, L0_xattn_bk, L0_xattn_Wv, L0_xattn_bv, L0_xattn_Wo, L0_xattn_bo, L0_ffn_W_fc, L0_ffn_ln_w, L0_ffn_ln_b, L0_ffn_W_proj, L1_xattn_Wq, L1_xattn_Wk, L1_xattn_Wv, L1_xattn_Wo, L1_xattn_bo, L1_ffn_router_w, L1_ffn_w1, L1_ffn_w3, L1_ffn_w2):
    import jax
    import jax.numpy as jnp

    def _L0_xattn_ref(q, k, v, attention_mask, Wq, bq, Wk, bk, Wv, bv, Wo, bo):
        import jax, jax.numpy as jnp
        import numpy as np
        N_HEADS = 16
        D_MODEL = 128
        HEAD_DIM = D_MODEL // N_HEADS
        MASK_FILL = -100000000.0

        def _split_heads(x):
            B, S, _ = x.shape
            return x.reshape(B, S, N_HEADS, HEAD_DIM).transpose(0, 2, 1, 3)
        qm = _split_heads(q @ Wq.T + bq)
        km = _split_heads(k @ Wk.T + bk)
        vm = _split_heads(v @ Wv.T + bv)
        scores = jnp.einsum('bnlh,bnph->bnlp', qm, km) / np.sqrt(HEAD_DIM).astype(np.float32)
        mask = attention_mask[:, None, None, :]
        scores = jnp.where(mask, scores, MASK_FILL)
        attn = jax.nn.softmax(scores, axis=-1)
        out = jnp.einsum('bnlp,bnph->bnlh', attn, vm)
        B, _, L, _ = out.shape
        out = out.transpose(0, 2, 1, 3).reshape(B, L, D_MODEL)
        return out @ Wo.T + bo

    def _L0_ffn_ref(x, W_fc, ln_w, ln_b, W_proj):
        import jax, jax.numpy as jnp
        import numpy as np
        EPS = 1e-06
        LN_EPS = 1e-05

        def _absmean_core(W):
            gamma = jnp.mean(jnp.abs(W)) + EPS
            Ws = W / gamma
            Wq = jnp.sign(Ws) * jnp.minimum(jnp.round(jnp.abs(Ws)), 1.0)
            return (Wq, gamma)

        @jax.custom_vjp
        def absmean(W):
            return _absmean_core(W)[0]

        def _absmean_fwd(W):
            Wq, gamma = _absmean_core(W)
            return (Wq, gamma)

        def _absmean_bwd(gamma, g):
            return (g / gamma,)
        absmean.defvjp(_absmean_fwd, _absmean_bwd)

        def layernorm(x, w, b, eps=LN_EPS):
            mu = jnp.mean(x, axis=-1, keepdims=True)
            var = jnp.mean((x - mu) ** 2, axis=-1, keepdims=True)
            return (x - mu) * jax.lax.rsqrt(var + eps) * w + b
        h = jnp.einsum('btd,hd->bth', x, absmean(W_fc))
        h = jax.nn.gelu(h, approximate=False)
        h = layernorm(h, ln_w, ln_b)
        return jnp.einsum('bth,dh->btd', h, absmean(W_proj))

    def _L1_xattn_ref(value, key, query, mask, Wq, Wk, Wv, Wo, bo):
        import jax, jax.numpy as jnp
        import numpy as np
        D_MODEL = 128
        HEADS = 16
        D_K = D_MODEL // HEADS
        NEG_INF = -10000000000.0
        n, q_len, _ = query.shape
        q = (query @ Wq.T).reshape(n, q_len, HEADS, D_K)
        k = (key @ Wk.T).reshape(n, key.shape[1], HEADS, D_K)
        v = (value @ Wv.T).reshape(n, value.shape[1], HEADS, D_K)
        scores = jnp.einsum('nqhd,nkhd->nhqk', q, k)
        scores = jnp.where(mask == 0, jnp.float32(NEG_INF), scores)
        attn = jax.nn.softmax(scores / jnp.sqrt(jnp.float32(D_K)), axis=-1)
        out = jnp.einsum('nhql,nlhd->nqhd', attn, v).reshape(n, q_len, D_MODEL)
        return out @ Wo.T + bo

    def _L1_ffn_ref(inputs, router_w, w1, w3, w2):
        import jax, jax.numpy as jnp
        import numpy as np
        B, S, H, F, E, K = (2, 128, 128, 256, 8, 2)
        b, s, h = inputs.shape
        x = inputs.reshape(-1, h)
        logits = x @ router_w
        top_vals, top_idx = jax.lax.top_k(logits, K)
        importance = jax.nn.softmax(top_vals.astype(jnp.float32), axis=-1).astype(x.dtype)
        one_hot = top_idx[..., None] == jnp.arange(E)[None, None, :]
        combine = jnp.sum(jnp.where(one_hot, importance[..., None], 0.0), axis=1)
        gate = jax.nn.silu(jnp.einsum('th,ehf->etf', x, w1))
        up = jnp.einsum('th,ehf->etf', x, w3)
        expert_out = jnp.einsum('etf,efh->eth', gate * up, w2)
        out = jnp.einsum('te,eth->th', combine, expert_out)
        return out.reshape(b, s, h)
    x = x + jnp.tanh(g_xattn[0]) * _L0_xattn_ref(_layernorm(x, axis=-1), ctx_1024, ctx_1024, mask_BxS2_bf1, L0_xattn_Wq, L0_xattn_bq, L0_xattn_Wk, L0_xattn_bk, L0_xattn_Wv, L0_xattn_bv, L0_xattn_Wo, L0_xattn_bo)
    x = x + jnp.tanh(g_ffn[0]) * _L0_ffn_ref(_layernorm(x, axis=-1), L0_ffn_W_fc, L0_ffn_ln_w, L0_ffn_ln_b, L0_ffn_W_proj)
    x = x + jnp.tanh(g_xattn[1]) * _L1_xattn_ref(ctx_1024, ctx_1024, _layernorm(x, axis=-1), mask_Bx1xSxS2_ik1, L1_xattn_Wq, L1_xattn_Wk, L1_xattn_Wv, L1_xattn_Wo, L1_xattn_bo)
    x = x + jnp.tanh(g_ffn[1]) * _L1_ffn_ref(_layernorm(x, axis=-1), L1_ffn_router_w, L1_ffn_w1, L1_ffn_w3, L1_ffn_w2)
    return x

_drawn_inputs = setup_inputs


def setup_inputs(seed=0):
    import zlib

    import numpy as np

    out = dict(_drawn_inputs(seed))
    spreads = {'g_ffn': (-1.0, 0.6),
     'L0_xattn_bq': (0.0, 0.411),
     'L0_xattn_bk': (0.0, 2.0),
     'L0_xattn_bv': (0.0, 0.1),
     'L0_xattn_bo': (0.0, 0.1),
     'L0_ffn_ln_w': (1.0, 0.2),
     'L0_ffn_ln_b': (0.0, 0.1)}
    factors = {'L1_xattn_Wq': 4.263, 'L1_xattn_Wk': 4.244, 'L1_xattn_bo': 64.0}
    for name, (base, spread) in spreads.items():
        noise = np.random.default_rng([zlib.crc32(name.encode()), seed]).standard_normal(out[name].shape)
        drawn = base * np.exp(spread * noise) if base else spread * noise
        out[name] = jnp.asarray(drawn.astype(out[name].dtype))
    for name, factor in factors.items():
        out[name] = (out[name] * factor).astype(out[name].dtype)
    return out
```

```python
from contextlib import ExitStack

import concourse.bass as bass
from concourse import mybir
from concourse.alu_op_type import AluOpType as ALU

B, S, D = 16, 256, 128
S2 = 1601
H, DH = 16, 8
P = 128
QT = S // P
KT = -(-S2 // P)
S2P = KT * P
NT = B * QT
FF = 512
NE, FE = 8, 256
HP = H // 2

K_PARTS = (0, 1, 0, 1, 2, 0)
Q_PARTS = (0, 0, 1, 1, 0, 2)
NPROD = len(K_PARTS)
ROWS_OF_HEADS = 2 * DH
MAX_ROW = NPROD * ROWS_OF_HEADS
BIAS_ROW = MAX_ROW + 6

SCALE = float(DH) ** -0.5
LN_EPS = 1e-5
GAMMA_EPS = 1e-6
MASKED = -(2.0 ** 100)
PADDED = -(2.0 ** 120)

F32 = mybir.dt.float32
BF16 = mybir.dt.bfloat16
I32 = mybir.dt.int32
U8 = mybir.dt.uint8
ACT = mybir.ActivationFunctionType
AX = mybir.AxisListType

GROUPS = HP // 2
UNITS = GROUPS * KT * 2
HALF = UNITS // 2
KW = (401, 400, 400, 400)
KO = (0, 401, 801, 1201)
CHUNKS = HP * 2 * QT * 4
LAG = 3
NSB = 3
NPB = 4
NRB = 2


def chunks_at(u, after=None):
    return [n for n in range(CHUNKS) if n * 203 // CHUNKS // 2 == u
            and after in (None, n * 203 // CHUNKS % 2)]


def unit(u):
    g, r = divmod(u, 2 * KT)
    return g, r // 2, 2 * g + r % 2, r % 2


AT_EPI = (6, 9)
AT_MAX_B = 12
AT_EPI_T = 18
AT_EPI_W = 21
AT_XN = 25
AT_Q = 28
AT_KP = (31, 34, 37, 40)
AT_MAX_A = 54
AT_V = (60, 63, 66, 69)
AT_MASK = (72, 76, 80, 84)
AT_Q_HI, AT_Q_MID = 30, 36
AT_K_HI, AT_K_MID = 44, 56
VT = ((0, 4), (4, 8), (8, 12), (12, 13))


def layer_norm_stats(nc, block, x, bn, mv, ve, rstd, minus_half, ve_ready, rstd_ready, x_in=None):

    def on_vector(dve):
        if x_in is not None:
            dve.wait_ge(x_in, 16)
        for t in range(NT):
            nc.vector.bn_stats(bn[:, t, :], x[:, QT + t, :])
        dve.drain()
        for t in range(NT):
            nc.vector.bn_aggr(mv[:, t, :], bn[:, t, :])
        dve.drain()
        nc.vector.tensor_scalar(ve[:], mv[:, :, 1], LN_EPS, None, ALU.add).then_inc(ve_ready, 1)
        dve.wait_ge(rstd_ready, 1)

    def on_gpsimd(pool):
        nc.gpsimd.memset(minus_half[:], -0.5)
        pool.drain()
        pool.wait_ge(ve_ready, 1)
        nc.gpsimd.tensor_tensor(rstd[:], ve[:], minus_half[:], ALU.pow).then_inc(rstd_ready, 1)

    return on_vector, on_gpsimd


def attention(nc, layer, x, stats, ident, ident_bf, head_of, row_of, d, scratch):
    first = layer == 0
    with ExitStack() as ctx:
        def sb(name, shape, dt):
            return ctx.enter_context(nc.sbuf_tensor(f"a{layer}_{name}", shape, dt))

        def pb(name, shape, dt=F32):
            return ctx.enter_context(nc.psum_tensor(f"a{layer}_{name}", shape, dt))

        def sem(name):
            return ctx.enter_context(nc.semaphore(f"a{layer}_{name}"))

        bn, mv, ve, rstd, minus_half = stats
        kx = sb("kx", [P, 2, HP, S2P], BF16)
        qx = sb("qx", [P, 2, HP, 2, S], BF16)
        vx = sb("vx", [P, 2, KT, H, DH + 1], F32)
        ctxT = sb("ctxT", [P, 2, S2], F32)
        kf = sb("kf", [P, S2], F32)
        kr = sb("kr", [P, S2], F32)
        kparts = sb("kparts", [P, 3, S2], BF16)
        qf = sb("qf", [P, 2, S], F32)
        qr = sb("qr", [P, 2, S], F32)
        qparts = sb("qparts", [P, 3, 2, S], BF16)
        probs = sb("probs", [P, NPB, 2 * S], F32)
        outT = sb("outT", [P, GROUPS, S], F32)
        attn = sb("attn", [P, QT, D], F32)
        attnT = sb("attnT", [P, S], F32)
        rsum = sb("rsum", [P, QT, H], F32)
        step = sb("step", [P, QT, D], F32)
        xn = sb("xn", [P, QT, D], F32)
        xnT = sb("xnT", [P, S], F32)
        mx = sb("mx", [P, QT, HP, 2, 4], F32)
        nm = sb("nm", [P, QT, HP // 2, 2], F32)
        nr = sb("nr", [P, QT, HP // 2, 2], F32)
        nparts = sb("nparts", [P, QT, HP // 2, 2, 3], BF16)
        wq = sb("wq", [P, D], F32)
        wk = sb("wk", [P, D], F32)
        wv = sb("wv", [P, D], F32)
        wo = sb("wo", [P, D], F32)
        bo = sb("bo", [P, D], F32)
        gate = sb("gate", [P, 1], F32)
        tgate = sb("tgate", [P, 1], F32)
        bk = sb("bk", [P, 1], F32)
        bq = sb("bq", [P, 1], F32)
        bq2 = sb("bq2", [P, 2], F32)
        if first:
            bv = sb("bv", [P, D], F32)
            keep = sb("keep", [P, S2], BF16)
            all_keep = sb("all_keep", [B, S2], U8)
            ones_kept = sb("ones_kept", [B, S2], BF16)
            bias = sb("bias", [B + 1, S2P], BF16)
        else:
            mask_in = sb("mask_in", [P, QT, S2], I32)
            mbias = sb("mbias", [P, 2, QT, S2], BF16)
            mbiasT = sb("mbiasT", [P, 2, KT, S], BF16)
            masked = sb("masked", [P, 2, KW[0]], BF16)

        rowmax = [pb(f"rowmax{i}", [P, 512]) for i in range(NRB)]
        scores = [pb(f"scores{i}", [P, 512]) for i in range(NSB)]
        pv = [pb(f"pv{i}", [P, 512]) for i in range(2)]
        shared = pb("shared", [P, 512])
        shared_bf = shared[:, :].bitcast(BF16)

        loaded = sem("loaded")
        x_in = sem("x_in")
        zeroed = sem("zeroed")
        zeros_kept = sem("zeros_kept")
        bias_ready = sem("bias_ready")
        ready = sem("ready")
        ve_ready, rstd_ready = sem("ve_ready"), sem("rstd_ready")
        scores_ready = sem("scores_ready")
        probs_ready = sem("probs_ready")
        probs_used = sem("probs_used")
        tail_ready = sem("tail_ready")
        tail_used = sem("tail_used")
        rowmax_ready = sem("rowmax_ready")
        rowmax_read = sem("rowmax_read")
        shared_act = sem("shared_act")
        shared_dve = sem("shared_dve")
        shared_read = sem("shared_read")
        group_copied = sem("group_copied")
        half_done = sem("half_done")
        parts_in = [sem("parts_in0"), sem("parts_in1")]
        ctx_in = [sem("ctx_in0"), sem("ctx_in1")]
        mask_landed = sem("mask_landed")
        mbias_ready = sem("mbias_ready")
        mbias_free = sem("mbias_free")
        kf_ready = sem("kf_ready")
        km_ready = sem("km_ready")
        khi_ready = sem("khi_ready")
        kr_ready = sem("kr_ready")
        kmid_ready = sem("kmid_ready")
        ksplit = sem("ksplit")
        qhi_ready = sem("qhi_ready")
        qr_ready = sem("qr_ready")
        qmid_ready = sem("qmid_ready")
        qsplit = sem("qsplit")
        staged = sem("staged")
        parts_free = sem("parts_free")
        xn_ready = sem("xn_ready")
        attn_ready = sem("attn_ready")
        nparts_ready = sem("nparts_ready")

        kscr, qscr, bscr, keepscr = scratch
        NPARTS_DMA = 16 * (2 * NPROD + 2)

        with nc.Block() as block:
            stats_dve, stats_pool = layer_norm_stats(nc, block, x, bn, mv, ve, rstd, minus_half,
                                                     ve_ready, rstd_ready, x_in if first else None)

            @block.sync
            def _(sp):
                n = 0
                if first:
                    sp.dma_start(x[:, QT:, :], d["x"].rearrange("b (t p) c -> p (b t) c", p=P)).then_inc(x_in, 16)
                    sp.dma_start(all_keep[:, :], d["keep"]).then_inc(loaded, 16)
                    sp.dma_start(bv[:, :], d["bv"].partition_broadcast(P)).then_inc(loaded, 16)
                    sp.dma_start(bq[:, :], d["bq"]).then_inc(loaded, 16)
                    sp.dma_start(bk[:, :], d["bk"]).then_inc(loaded, 16)
                    n = 4
                for w, name in ((wq, "wq"), (wk, "wk"), (wv, "wv"), (wo, "wo")):
                    sp.dma_start(w[:, :], d[name]).then_inc(loaded, 16)
                sp.dma_start(bo[:, :], d["bo"].partition_broadcast(P)).then_inc(loaded, 16)
                sp.dma_start(gate[:, :], d["gate"].partition_broadcast(P)).then_inc(loaded, 16)
                sp.wait_ge(loaded, 16 * (n + 6))
                sp.wait_ge(zeroed, 1)
                for par in range(2):
                    sp.dma_start(qscr[par, 3].rearrange("p c q -> (p c) q"), qparts[:, 0].rearrange("p j q -> p (j q)"))\
                      .then_inc(zeros_kept, 16)
                if first:
                    sp.wait_ge(bias_ready, 1)
                    sp.dma_start(bscr, bias[:, :]).then_inc(zeros_kept, 16)
                    sp.dma_start(keepscr, ones_kept[:, :]).then_inc(zeros_kept, 16)
                    sp.wait_ge(zeros_kept, 64)
                else:
                    sp.wait_ge(zeros_kept, 32)

            @block.vector
            def _(dve):
                nc.vector.memset(kx[:], 0.0)
                nc.vector.memset(pv[0][:], 0.0)
                nc.vector.memset(pv[1][:], 0.0)
                nc.vector.memset(probs[:], 1.0)
                nc.vector.memset(outT[:], 1.0)
                dve.drain()
                nc.vector.memset(qparts[:], 0.0).then_inc(zeroed, 1)
                if first:
                    nc.vector.memset(bias[:], 0.0)
                    dve.drain()
                    nc.vector.memset(bias[:, S2:S2P], PADDED)
                    dve.wait_ge(loaded, 16 * 10)
                    nc.vector.tensor_copy(ones_kept[:, :], all_keep[:, :])
                    nc.vector.tensor_scalar(bias[0:B, 0:S2], all_keep[:, :], -1.0, -MASKED,
                                            ALU.add, ALU.mult)
                    dve.drain()
                    nc.vector.tensor_scalar(bq2[:, :], head_of[:, :], bq[:, 0:1], None, ALU.mult)\
                        .then_inc(bias_ready, 1)
                else:
                    nc.vector.memset(bk[:], 0.0)
                    nc.vector.memset(bq2[:], 0.0)
                stats_dve(dve)

            @block.scalar
            def _(act):
                act.wait_ge(loaded, 16 * (10 if first else 6))
                nc.scalar.activation(tgate[:, :], gate[:, :], ACT.Tanh)

            @block.gpsimd
            def _(pool):
                nc.gpsimd.memset(qx[:], 0.0)
                nc.gpsimd.memset(vx[:], 0.0)
                if not first:
                    nc.gpsimd.memset(mbiasT[:], 0.0)
                pool.drain()
                nc.gpsimd.memset(vx[:, :, 0:KT - 1, :, DH:DH + 1], 1.0)
                pool.drain()
                nc.gpsimd.memset(vx[0:S2 - (KT - 1) * P, :, KT - 1, :, DH:DH + 1], 1.0)
                pool.drain()
                nc.gpsimd.memset(qx[MAX_ROW:BIAS_ROW + 1], 1.0)
                pool.drain()
                nc.gpsimd.memset(qx[MAX_ROW:BIAS_ROW], 0.0)
                pool.wait_ge(zeroed, 1)
                pool.drain()
                nc.gpsimd.memset(kx[MAX_ROW:BIAS_ROW], 1.0)
                pool.drain()
                stats_pool(pool)


        def pe_body(par, exp, mx_on, prep, vals, epi):
            nxt = 1 - par
            rounds = [0]

            def shared_free():
                if rounds[0]:
                    pe.wait_ge(shared_read, rounds[0])
                rounds[0] += 1

            def qk(u):
                g, t, p, _ = unit(u)
                out = scores[u % NSB][:, :]
                mm = nc.tensor.matmul(out, kx[:, par, p, t * P:(t + 1) * P], qx[:, par, p, :, :],
                                      start=True, stop=first)
                if not first:
                    mm = nc.tensor.matmul(out, ident_bf[:, :],
                                          mbiasT[:, par, t:t + 1, :].broadcast_to([P, 2, S]),
                                          start=False, stop=True)
                mm.then_inc(scores_ready, 1)

            def values(u, of=par):
                g, t, p, a = unit(u)
                if t == 0 and a == 0:
                    if g == 0:
                        pe.wait_ge(group_copied, GROUPS - 1)
                    if g >= 2:
                        pe.wait_ge(group_copied, g - 1)
                for j in range(2):
                    row = 32 * (2 * a + j)
                    mm = nc.tensor.matmul(pv[g % 2][row:row + DH + 1, 0:S], vx[:, of, t, 2 * p + j, :],
                                          probs[:, u % NPB, j * S:(j + 1) * S],
                                          start=(t == 0), stop=(t == KT - 1), skip_group_check=True)
                    if j == 0 and u in (HALF - LAG + 1, UNITS - LAG - 1):
                        mm.then_inc(half_done, 1)
                mm.then_inc(probs_used if u < UNITS - LAG else tail_used, 1)

            def chunk(n):
                p, j, qt, c = n // 16, n // 8 % 2, n // 4 % 2, n % 4
                if n == 0:
                    pe.wait_ge(parts_in[0], NPARTS_DMA)
                    pe.sem_inc(parts_in[0], -NPARTS_DMA)
                if n == CHUNKS // 2:
                    pe.wait_ge(parts_in[1], NPARTS_DMA)
                    pe.sem_inc(parts_in[1], -NPARTS_DMA)
                if n >= NRB:
                    pe.wait_ge(rowmax_read, n - NRB + 1)
                nc.tensor.matmul(rowmax[n % NRB][:, 0:KW[c]], qx[:, nxt, p, j, qt * P:(qt + 1) * P],
                                 kx[:, nxt, p, KO[c]:KO[c] + KW[c]], start=True, stop=True)\
                    .then_inc(rowmax_ready, 1)
                if not exp and n in (1, CHUNKS // 2 + 1):
                    pe.drain().then_inc(half_done, 1)

            def put_maxima(par_of, half, waits):
                pe.wait_ge(nparts_ready, waits)
                shared_free()
                for p in range(HP // 2):
                    for qt in range(QT):
                        o = (p * QT + qt) * P
                        mm = nc.tensor.transpose(shared_bf[0:6, o:o + P],
                                                 nparts[:, qt, p, :, :], ident_bf[:, :])
                mm.then_inc(shared_act, 1)

            nmax = [0]
            for u in range(UNITS):
                if epi and u < LAG:
                    pe.wait_ge(tail_ready, min(u + 2, LAG))
                    if u == LAG - 1:
                        pe.sem_inc(tail_ready, -LAG)
                if exp and u >= LAG:
                    pe.wait_ge(probs_ready, u - LAG + 1)
                if exp:
                    qk(u)
                if mx_on:
                    for n in chunks_at(u, 0):
                        chunk(n)
                if epi and u < LAG:
                    values(UNITS - LAG + u, nxt)
                if exp and u >= LAG:
                    values(u - LAG)
                if mx_on:
                    for n in chunks_at(u, 1):
                        chunk(n)
                if epi and u == AT_EPI[0]:
                    pe.wait_ge(group_copied, GROUPS)
                    pe.sem_inc(group_copied, -GROUPS)
                if epi and u in AT_EPI:
                    qt = AT_EPI.index(u)
                    shared_free()
                    for g in range(GROUPS):
                        mm = nc.tensor.transpose(shared[:, g * P:(g + 1) * P],
                                                 outT[:, g, qt * P:(qt + 1) * P], ident[:, :])
                    mm.then_inc(shared_dve, 1)
                if exp and u == AT_MAX_B:
                    nmax[0] += 1
                    put_maxima(par, 1, nmax[0])
                if epi and u == AT_EPI_T:
                    pe.wait_ge(attn_ready, 1)
                    shared_free()
                    for qt in range(QT):
                        mm = nc.tensor.transpose(shared[:, qt * P:(qt + 1) * P], attn[:, qt, :], ident[:, :])
                    mm.then_inc(shared_act, 1)
                if epi and u == AT_EPI_W:
                    shared_free()
                    for qt in range(QT):
                        mm = nc.tensor.matmul(shared[:, qt * P:(qt + 1) * P],
                                              attnT[:, qt * P:(qt + 1) * P], wo[:, :], start=True, stop=True)
                    mm.then_inc(shared_dve, 1)
                if prep and u == AT_XN:
                    pe.wait_ge(xn_ready, 1)
                    shared_free()
                    for qt in range(QT):
                        mm = nc.tensor.transpose(shared[:, qt * P:(qt + 1) * P], xn[:, qt, :], ident[:, :])
                    mm.then_inc(shared_act, 1)
                if prep and u == AT_Q:
                    shared_free()
                    nc.tensor.matmul(shared[:, 0:S], wq[:, :], xnT[:, :], start=True, stop=True)\
                        .then_inc(shared_act, 1)
                if prep and u in AT_KP:
                    i = AT_KP.index(u)
                    if i == 0:
                        pe.wait_ge(ctx_in[par], 16)
                        pe.sem_inc(ctx_in[par], -16)
                    shared_free()
                    nc.tensor.matmul(shared[:, 0:KW[i]], wk[:, :], ctxT[:, par, KO[i]:KO[i] + KW[i]],
                                     start=True, stop=True).then_inc(shared_act, 1)
                if mx_on and u == AT_MAX_A:
                    nmax[0] += 1
                    put_maxima(nxt, 0, nmax[0])
                if vals and u in AT_V:
                    shared_free()
                    for t in range(*VT[AT_V.index(u)]):
                        w = min(P, S2 - t * P)
                        o = t % 4 * P
                        mm = nc.tensor.matmul(shared[0:w, o:o + D], ctxT[:, nxt, t * P:t * P + w],
                                              wv[:, :], start=True, stop=True)
                    mm.then_inc(shared_act, 1)
                if vals and not first and u in AT_MASK:
                    shared_free()
                    for t in range(*VT[AT_MASK.index(u)]):
                        w = min(P, S2 - t * P)
                        for qt in range(QT):
                            o = (t % 4 * QT + qt) * P
                            mm = nc.tensor.transpose(shared_bf[0:w, o:o + P],
                                                     mbias[:, nxt, qt, t * P:t * P + w], ident_bf[:, :])
                    mm.then_inc(shared_act, 1)
            if mx_on and not exp:
                pe.drain().then_inc(half_done, 1)
            if exp:
                pe.sem_inc(probs_ready, -(UNITS - LAG))
            if mx_on:
                pe.wait_ge(rowmax_read, CHUNKS)
                pe.sem_inc(rowmax_read, -CHUNKS)
            if rounds[0]:
                pe.wait_ge(shared_read, rounds[0])
                pe.sem_inc(shared_read, -rounds[0])
            if nmax[0]:
                pe.sem_inc(nparts_ready, -nmax[0])
            if epi:
                pe.sem_inc(attn_ready, -1)
            if prep:
                pe.sem_inc(xn_ready, -1)

        def act_body(par, exp, mx_on, prep, vals, epi):
            nxt = 1 - par
            rounds = [0]

            def shared_full():
                rounds[0] += 1
                act.wait_ge(shared_act, rounds[0])

            def put_maxima(par_of, half, i):
                if i == 0:
                    shared_full()
                j, pp = i // 2, i % 2
                ins = nc.scalar.activation(
                    qx[MAX_ROW:BIAS_ROW, par_of, 4 * half + 2 * pp:4 * half + 2 * pp + 2, j, :],
                    shared_bf[0:6, 512 * pp:512 * (pp + 1)].rearrange("r (p q) -> r p q", q=S), ACT.Copy,
                    scale=row_of[0:6, j:j + 1])
                if i == 3:
                    ins.then_inc(shared_read, 1)

            def group(g):
                if g < GROUPS - 1:
                    act.wait_ge(probs_used, 2 * KT * (g + 1))
                else:
                    act.wait_ge(tail_used, LAG)
                    act.sem_inc(tail_used, -LAG)
                nc.scalar.copy(outT[:, g, :], pv[g % 2][:, 0:S]).then_inc(group_copied, 1)

            if epi:
                act.wait_ge(probs_used, UNITS - LAG)
                act.sem_inc(probs_used, -(UNITS - LAG))
            for u in range(UNITS):
                if exp:
                    act.wait_ge(scores_ready, u + 1)
                    if u >= NPB:
                        act.wait_ge(probs_used, u - NPB + 1)
                    elif epi and u:
                        act.wait_ge(tail_used, u)
                    nc.scalar.activation(probs[:, u % NPB, :], scores[u % NSB][:, :], ACT.Exp, scale=SCALE)\
                        .then_inc(probs_ready if u < UNITS - LAG else tail_ready, 1)
                if epi and u == NPB - 1:
                    group(GROUPS - 1)
                if exp and u > LAG + 1 and (u - LAG - 1) % (2 * KT) == 2 * KT - 1:
                    group((u - LAG - 1) // (2 * KT))
                if exp and AT_MAX_B <= u < AT_MAX_B + 4:
                    put_maxima(par, 1, u - AT_MAX_B)
                if epi and u == AT_EPI_T:
                    shared_full()
                    nc.scalar.copy(attnT[:, :], shared[:, 0:S]).then_inc(shared_read, 1)
                if prep and u == AT_XN:
                    shared_full()
                    nc.scalar.copy(xnT[:, :], shared[:, 0:S]).then_inc(shared_read, 1)
                if prep and u == AT_Q:
                    shared_full()
                    for j in range(2):
                        ins = nc.scalar.activation(qf[:, j, :], shared[:, 0:S], ACT.Identity,
                                                   scale=head_of[:, j:j + 1], bias=bq2[:, j:j + 1])
                    ins.then_inc(shared_read, 1)
                if prep and u == AT_Q_HI:
                    act.wait_ge(parts_free, 1)
                    act.sem_inc(parts_free, -1)
                    act.drain()
                    nc.scalar.copy(qparts[:, 0], qf[:, :, :]).then_inc(qhi_ready, 1)
                if prep and u == AT_Q_MID:
                    act.wait_ge(qr_ready, 1)
                    act.sem_inc(qr_ready, -1)
                    nc.scalar.copy(qparts[:, 1], qr[:, :, :]).then_inc(qmid_ready, 1)
                if prep and u in AT_KP:
                    i = AT_KP.index(u)
                    shared_full()
                    nc.scalar.activation(kf[:, KO[i]:KO[i] + KW[i]], shared[:, 0:KW[i]], ACT.Identity,
                                         bias=bk[:, 0:1]).then_inc(shared_read, 1)
                    if i == 3:
                        act.drain().then_inc(kf_ready, 1)
                if prep and AT_K_HI <= u < AT_K_HI + 4:
                    i = u - AT_K_HI
                    if first and i == 0:
                        act.wait_ge(km_ready, 1)
                        act.sem_inc(km_ready, -1)
                    ins = nc.scalar.copy(kparts[:, 0, KO[i]:KO[i] + KW[i]], kf[:, KO[i]:KO[i] + KW[i]])
                    if i == 3:
                        ins.then_inc(khi_ready, 1)
                if prep and AT_K_MID <= u < AT_K_MID + 4:
                    i = u - AT_K_MID
                    if i == 0:
                        act.wait_ge(kr_ready, 1)
                        act.sem_inc(kr_ready, -1)
                    ins = nc.scalar.copy(kparts[:, 1, KO[i]:KO[i] + KW[i]], kr[:, KO[i]:KO[i] + KW[i]])
                    if i == 3:
                        ins.then_inc(kmid_ready, 1)
                if mx_on and AT_MAX_A <= u < AT_MAX_A + 4:
                    put_maxima(nxt, 0, u - AT_MAX_A)
                if vals and u in AT_V:
                    a, b = VT[AT_V.index(u)]
                    w = min(P, S2 - a * P)
                    shared_full()
                    nc.scalar.copy(vx[0:w, nxt, a:b, :, 0:DH],
                                   shared[0:w, 0:(b - a) * D].rearrange("k (t h e) -> k t h e", h=H, e=DH))\
                        .then_inc(shared_read, 1)
                if vals and not first and u in AT_MASK:
                    a, b = VT[AT_MASK.index(u)]
                    w = min(P, S2 - a * P)
                    shared_full()
                    nc.scalar.copy(mbiasT[0:w, nxt, a:b, :],
                                   shared_bf[0:w, 0:(b - a) * S].rearrange("k (t q) -> k t q", q=S))\
                        .then_inc(shared_read, 1)
            if exp:
                act.sem_inc(scores_ready, -UNITS)
            if rounds[0]:
                act.sem_inc(shared_act, -rounds[0])

        def dve_body(par, exp, mx_on, prep, vals, epi, b):
            nxt = 1 - par
            rounds = [0]

            def shared_full():
                rounds[0] += 1
                dve.wait_ge(shared_dve, rounds[0])

            def split_maxima(half):
                dve.drain()
                nc.vector.tensor_reduce(nm[:], mx[:, :, 4 * half:4 * half + 4, :, :], AX.X, ALU.max, negate=True)
                dve.drain()
                nc.vector.tensor_copy(nparts[:, :, :, :, 0], nm[:])
                dve.drain()
                nc.vector.tensor_tensor(nr[:], nm[:], nparts[:, :, :, :, 0], ALU.subtract)
                dve.drain()
                nc.vector.tensor_copy(nparts[:, :, :, :, 1], nr[:])
                dve.drain()
                nc.vector.tensor_tensor(nparts[:, :, :, :, 2], nr[:], nparts[:, :, :, :, 1], ALU.subtract)\
                    .then_inc(nparts_ready, 1)

            if exp:
                split_maxima(1)
            for u in range(UNITS):
                if mx_on:
                    for n in chunks_at(u):
                        p, j, qt, c = n // 16, n // 8 % 2, n // 4 % 2, n % 4
                        dve.wait_ge(rowmax_ready, n + 1)
                        src, dst = rowmax[n % NRB][:, 0:KW[c]], mx[:, qt, p, j, c:c + 1]
                        if first:
                            nc.vector.tensor_reduce(dst, src, AX.X, ALU.max).then_inc(rowmax_read, 1)
                        else:
                            if n == 0:
                                dve.wait_ge(mbias_ready, 1)
                                dve.sem_inc(mbias_ready, -1)
                            nc.vector.tensor_tensor_reduce(masked[:, n % 2, 0:KW[c]], src,
                                                           mbias[:, nxt, qt, KO[c]:KO[c] + KW[c]], 1.0, PADDED, ALU.add, ALU.max, dst)\
                                .then_inc(rowmax_read, 1)
                    if CHUNKS // 2 - 1 in chunks_at(u):
                        split_maxima(0)
                if epi and u in AT_EPI:
                    qt = AT_EPI.index(u)
                    shared_full()
                    full = shared[:, :].rearrange("q (h e) -> q h e", e=32)
                    nc.vector.reciprocal(rsum[:, qt, :], full[:, :, DH])
                    dve.drain()
                    o = attn[:, qt, :].rearrange("q (h e) -> q h e", e=DH)
                    ins = nc.vector.tensor_tensor(o, full[:, :, 0:DH],
                                                  rsum[:, qt, :].unsqueeze(2).broadcast_to([P, H, DH]), ALU.mult)
                    ins.then_inc(shared_read, 1)
                    dve.drain()
                    if first:
                        ins = nc.vector.tensor_tensor(attn[:, qt, :], attn[:, qt, :], bv[:, :], ALU.add)
                        if qt == 1:
                            ins.then_inc(attn_ready, 1)
                    elif qt == 1:
                        dve.drain().then_inc(attn_ready, 1)
                if epi and u == AT_EPI_W:
                    shared_full()
                    nc.vector.tensor_tensor(step[:], shared[:, 0:S].rearrange("q (t c) -> q t c", t=QT),
                                            bo[:, :].unsqueeze(1).broadcast_to([P, QT, D]), ALU.add)\
                        .then_inc(shared_read, 1)
                    dve.drain()
                    at = x[:, bass.ds(b * QT, QT), :]
                    nc.vector.scalar_tensor_tensor(out=at, in0=step[:], scalar=tgate[:, 0:1], in1=at,
                                                   op0=ALU.mult, op1=ALU.add)
                if prep and u == AT_EPI_W + 1:
                    for qt in range(QT):
                        ins = nc.vector.tensor_scalar(xn[:, qt, :],
                                                      x[:, bass.ds((b + 3) * QT + qt, 1), :].rearrange("p a c -> p (a c)"),
                                                      mv[:, bass.ds((b + 2) * QT + qt, 1), 0],
                                                      rstd[:, bass.ds((b + 2) * QT + qt, 1)],
                                                      ALU.subtract, ALU.mult)
                    ins.then_inc(xn_ready, 1)
            if rounds[0]:
                dve.sem_inc(shared_dve, -rounds[0])
            if mx_on:
                dve.sem_inc(rowmax_ready, -CHUNKS)
                if not first:
                    dve.drain().then_inc(mbias_free, 1)

        def pool_body(par, exp, mx_on, prep, vals, epi):
            if not prep:
                return
            if not first:
                pool.wait_ge(mask_landed, 16)
                pool.sem_inc(mask_landed, -16)
                pool.wait_ge(mbias_free, 1)
                pool.sem_inc(mbias_free, -1)
                for qt in range(QT):
                    ins = nc.gpsimd.tensor_scalar(mbias[:, par, qt, :], mask_in[:, qt, :], 0.0, MASKED,
                                                  ALU.is_equal, ALU.mult)
                ins.then_inc(mbias_ready, 1)
            pool.wait_ge(qhi_ready, 1)
            pool.sem_inc(qhi_ready, -1)
            nc.gpsimd.tensor_tensor(qr[:, :, :], qf[:, :, :], qparts[:, 0], ALU.subtract).then_inc(qr_ready, 1)
            pool.wait_ge(qmid_ready, 1)
            pool.sem_inc(qmid_ready, -1)
            nc.gpsimd.tensor_tensor(qparts[:, 2], qr[:, :, :], qparts[:, 1], ALU.subtract).then_inc(qsplit, 1)
            pool.wait_ge(kf_ready, 1)
            pool.sem_inc(kf_ready, -1)
            if first:
                pool.wait_ge(mask_landed, 16)
                pool.sem_inc(mask_landed, -16)
                nc.gpsimd.tensor_tensor(kf[:, :], kf[:, :], keep[:, :], ALU.mult).then_inc(km_ready, 1)
            pool.wait_ge(khi_ready, 1)
            pool.sem_inc(khi_ready, -1)
            if first:
                pool.drain()
            nc.gpsimd.tensor_tensor(kr[:, :], kf[:, :], kparts[:, 0, :], ALU.subtract).then_inc(kr_ready, 1)
            pool.wait_ge(kmid_ready, 1)
            pool.sem_inc(kmid_ready, -1)
            pool.drain()
            nc.gpsimd.tensor_tensor(kparts[:, 2, :], kr[:, :], kparts[:, 1, :], ALU.subtract).then_inc(ksplit, 1)

        def sp_body(par, exp, mx_on, prep, vals, epi, b):
            if prep:
                sp.dma_start(ctxT[:, par, :], d["ctxT"][bass.ds(b + 2, 1)].rearrange("a p k -> p (a k)"))\
                    .then_inc(ctx_in[par], 16)
                if first:
                    sp.dma_start(keep[:, :], keepscr[bass.ds(b + 2, 1), :].broadcast_to([P, S2]))\
                        .then_inc(mask_landed, 16)
                else:
                    sp.dma_start(mask_in[:, :, :], d["mask"][bass.ds(b + 2, 1)]
                                 .rearrange("a (t p) k -> p (a t) k", p=P)).then_inc(mask_landed, 16)
                sp.wait_ge(qsplit, 1)
                sp.sem_inc(qsplit, -1)
                sp.dma_start(qscr[par, 0:3].rearrange("s p c q -> (p c) s q"),
                             qparts[:].rearrange("p s j q -> p s (j q)")).then_inc(staged, 16)
                sp.wait_ge(ksplit, 1)
                sp.sem_inc(ksplit, -1)
                sp.dma_start(kscr[par].rearrange("s p c k -> (p c) s k"), kparts[:, :, :]).then_inc(staged, 16)
                sp.wait_ge(staged, 32)
                sp.sem_inc(staged, -32)
                sp.sem_inc(parts_free, 1)
            for half in range(2):
                if exp or mx_on:
                    sp.wait_ge(half_done, half + 1)
                if prep:
                    ps = slice(4 * half, 4 * half + 4)
                    for i in range(NPROD):
                        rows = slice(i * ROWS_OF_HEADS, (i + 1) * ROWS_OF_HEADS)
                        sp.dma_start(kx[rows, par, ps, 0:S2], kscr[par, K_PARTS[i], ps].rearrange("p c k -> c p k"))\
                            .then_inc(parts_in[half], 16)
                        sp.dma_start(qx[rows, par, ps].rearrange("c p j q -> c p (j q)"),
                                     qscr[par, Q_PARTS[i], ps].rearrange("p c q -> c p q"))\
                            .then_inc(parts_in[half], 16)
                    sp.dma_start(qx[MAX_ROW:BIAS_ROW, par, ps].rearrange("c p j q -> c p (j q)"),
                                 qscr[par, 3, ps, 0:6].rearrange("p c q -> c p q")).then_inc(parts_in[half], 16)
                    row = bass.ds(b + 2, 1) if first else slice(B, B + 1)
                    sp.dma_start(kx[BIAS_ROW:BIAS_ROW + 1, par, ps, :],
                                 bscr[row, :].unsqueeze(1).broadcast_to([1, 4, S2P]))\
                        .then_inc(parts_in[half], 16)
            if exp:
                sp.sem_inc(half_done, -2)
            elif mx_on:
                sp.wait_ge(half_done, 3)
                sp.sem_inc(half_done, -3)

        pe = act = dve = pool = sp = None

        before = [(-2, dict(exp=0, mx_on=0, prep=1, vals=0, epi=0)),
                  (-1, dict(exp=0, mx_on=1, prep=1, vals=1, epi=0))]
        steady = dict(exp=1, mx_on=1, prep=1, vals=1, epi=1)
        after = [(B - 2, dict(exp=1, mx_on=1, prep=0, vals=1, epi=1)),
                 (B - 1, dict(exp=1, mx_on=0, prep=0, vals=0, epi=1)),
                 (B, dict(exp=0, mx_on=0, prep=0, vals=0, epi=1))]

        def whole(eng, body, with_batch):
            def one(b, par, flags):
                if with_batch:
                    body(par, b=b, **flags)
                else:
                    body(par, **flags)
            for b, flags in before:
                one(b, b % 2, flags)
            with eng.Fori(0, (B - 2) // 2) as i:
                for par in range(2):
                    one(i * 2 + par, par, steady)
            for b, flags in after:
                one(b, b % 2, flags)

        with nc.Block() as block:
            @block.tensor
            def _(eng):
                nonlocal pe
                pe = eng
                pe.sem_inc(probs_used, UNITS - LAG)
                whole(eng, pe_body, False)

            @block.scalar
            def _(eng):
                nonlocal act
                act = eng
                act.sem_inc(tail_ready, LAG)
                act.sem_inc(group_copied, GROUPS - 1)
                whole(eng, act_body, False)

            @block.vector
            def _(eng):
                nonlocal dve
                dve = eng
                whole(eng, dve_body, True)

            @block.gpsimd
            def _(eng):
                nonlocal pool
                pool = eng
                pool.sem_inc(mbias_free, 2)
                whole(eng, pool_body, False)

            @block.sync
            def _(eng):
                nonlocal sp
                sp = eng
                sp.sem_inc(parts_free, 1)
                whole(eng, sp_body, True)
                sp.drain()


def ternary_ffn(nc, x, stats, ident, d):
    FC = FF // P
    LANES = 4
    with ExitStack() as ctx:
        def sb(name, shape, dt=F32):
            return ctx.enter_context(nc.sbuf_tensor(f"f0_{name}", shape, dt))

        def sem(name):
            return ctx.enter_context(nc.semaphore(f"f0_{name}"))

        bn, mv, ve, rstd, minus_half = stats
        w = [sb("w_fc", [P, FF]), sb("w_proj", [P, FC, D])]
        flat = [w[0][:, :], w[1][:, :, :].rearrange("p c d -> p (c d)")]
        mag = sb("mag", [P, 2, FF])
        neg = sb("neg", [P, 2, FF])
        part = sb("part", [P, 2])
        gam = sb("gam", [P, 2])
        rgam = sb("rgam", [P, 2])
        ones = sb("ones", [P, P])
        lw = sb("lw", [P, FC])
        lb = sb("lb", [P, FC])
        gate = sb("gate", [P, 1])
        tgate = sb("tgate", [P, 1])
        xn = sb("xn", [P, LANES, D])
        xnT = sb("xnT", [P, LANES, P])
        h = sb("h", [P, LANES, FF])
        hn = sb("hn", [P, LANES, FF])
        hT = sb("hT", [P, LANES, FC, P])
        hbn = sb("hbn", [P, LANES, 6])
        hmv = sb("hmv", [P, LANES, 2])
        hve = sb("hve", [P, LANES])
        hrs = sb("hrs", [P, LANES])
        pa = [ctx.enter_context(nc.psum_tensor(f"f0_pa{i}", [P, 512], F32)) for i in range(LANES)]
        pb = [ctx.enter_context(nc.psum_tensor(f"f0_pb{i}", [P, 512], F32)) for i in range(LANES)]

        loaded, mag_ready, sums_ready, gam_ready = sem("loaded"), sem("mag_ready"), sem("sums_ready"), sem("gam_ready")
        ve_ready, rstd_ready = sem("ve_ready"), sem("rstd_ready")
        w_ready = sem("w_ready")
        xn_ready = sem("xn_ready")
        xnT_ready = sem("xnT_ready")
        xnT_copied = sem("xnT_copied")
        fc_ready = sem("fc_ready")
        gelu_ready = sem("gelu_ready")
        hve_ready = sem("hve_ready")
        hrs_ready = sem("hrs_ready")
        hn_ready = sem("hn_ready")
        hT_ready = sem("hT_ready")
        hT_copied = sem("hT_copied")
        proj_ready = sem("proj_ready")
        proj_read = sem("proj_read")

        with nc.Block() as block:
            stats_dve, stats_pool = layer_norm_stats(nc, block, x, bn, mv, ve, rstd, minus_half,
                                                     ve_ready, rstd_ready)

            @block.sync
            def _(sp):
                sp.dma_start(w[0][:, :], d["w_fcT"]).then_inc(loaded, 16)
                sp.dma_start(w[1][:, :, :], d["w_projT"].rearrange("(c p) d -> p c d", p=P)).then_inc(loaded, 16)
                sp.dma_start(lw[:, :], d["ln_w"]).then_inc(loaded, 16)
                sp.dma_start(lb[:, :], d["ln_b"]).then_inc(loaded, 16)
                sp.dma_start(gate[:, :], d["gate"].partition_broadcast(P)).then_inc(loaded, 16)

            @block.tensor
            def _(pe):
                pe.wait_ge(mag_ready, 1)
                nc.tensor.matmul(pa[0][:, 0:2], ones[:, :], part[:, :], start=True, stop=True)\
                    .then_inc(sums_ready, 1)
                pe.wait_ge(w_ready, 1)
                with pe.Fori(0, NT // LANES):
                    for i in range(LANES):
                        pe.wait_ge(xn_ready, i + 1)
                        nc.tensor.transpose(pa[i][:, 0:P], xn[:, i, :], ident[:, :]).then_inc(xnT_ready, 1)
                    for i in range(LANES):
                        pe.wait_ge(xnT_copied, i + 1)
                        nc.tensor.matmul(pb[i][:, :], xnT[:, i, :], w[0][:, :], start=True, stop=True)\
                            .then_inc(fc_ready, 1)
                    for i in range(LANES):
                        pe.wait_ge(hn_ready, i + 1)
                        for c in range(FC):
                            mm = nc.tensor.transpose(pa[i][:, c * P:(c + 1) * P],
                                                     hn[:, i, c * P:(c + 1) * P], ident[:, :])
                        mm.then_inc(hT_ready, 1)
                    for i in range(LANES):
                        pe.wait_ge(hT_copied, i + 1)
                        for c in range(FC):
                            mm = nc.tensor.matmul(pb[i][:, 0:D], hT[:, i, c, :], w[1][:, c, :],
                                                  start=(c == 0), stop=(c == FC - 1))
                        mm.then_inc(proj_ready, 1)
                    pe.wait_ge(proj_read, LANES)
                    for s in (xn_ready, xnT_copied, hn_ready, hT_copied, proj_read):
                        pe.sem_inc(s, -LANES)

            @block.scalar
            def _(act):
                act.wait_ge(loaded, 80)
                nc.scalar.activation(tgate[:, :], gate[:, :], ACT.Tanh)
                with act.Fori(0, NT // LANES):
                    for i in range(LANES):
                        act.wait_ge(xnT_ready, i + 1)
                        nc.scalar.copy(xnT[:, i, :], pa[i][:, 0:P]).then_inc(xnT_copied, 1)
                    for i in range(LANES):
                        act.wait_ge(fc_ready, i + 1)
                        nc.scalar.activation(h[:, i, :], pb[i][:, :], ACT.Gelu).then_inc(gelu_ready, 1)
                    for i in range(LANES):
                        act.wait_ge(hT_ready, i + 1)
                        for c in range(FC):
                            ins = nc.scalar.activation(hT[:, i, c, :], pa[i][:, c * P:(c + 1) * P], ACT.Identity,
                                                       scale=lw[:, c:c + 1], bias=lb[:, c:c + 1])
                        ins.then_inc(hT_copied, 1)
                    for s in (xnT_ready, fc_ready, hT_ready):
                        act.sem_inc(s, -LANES)

            @block.gpsimd
            def _(pool):
                stats_pool(pool)
                with pool.Fori(0, NT // LANES):
                    for i in range(LANES):
                        pool.wait_ge(hve_ready, i + 1)
                        nc.gpsimd.tensor_tensor(hrs[:, i:i + 1], hve[:, i:i + 1], minus_half[:, i:i + 1], ALU.pow)\
                            .then_inc(hrs_ready, 1)
                    pool.sem_inc(hve_ready, -LANES)

            def normalise(dve, i):
                dve.wait_ge(hrs_ready, i + 1)
                nc.vector.tensor_scalar(hn[:, i, :], h[:, i, :], hmv[:, i, 0:1], hrs[:, i:i + 1],
                                        ALU.subtract, ALU.mult).then_inc(hn_ready, 1)

            @block.vector
            def _(dve):
                nc.vector.memset(ones[:], 1.0)
                dve.wait_ge(loaded, 80)
                for i in range(2):
                    nc.vector.tensor_reduce(part[:, i:i + 1], flat[i], AX.X, ALU.add, apply_absolute_value=True)
                dve.drain().then_inc(mag_ready, 1)
                dve.wait_ge(sums_ready, 1)
                nc.vector.tensor_scalar(gam[:, :], pa[0][:, 0:2], 1.0 / (D * FF), GAMMA_EPS, ALU.mult, ALU.add)
                dve.drain()
                nc.vector.reciprocal(rgam[:, :], gam[:, :])
                dve.drain()
                for i in range(2):
                    nc.vector.tensor_scalar(mag[:, i, :], flat[i], rgam[:, i:i + 1], 0.5, ALU.mult, ALU.is_gt)
                    nc.vector.tensor_scalar(neg[:, i, :], flat[i], rgam[:, i:i + 1], -0.5, ALU.mult, ALU.is_lt)
                dve.drain()
                for i in range(2):
                    nc.vector.tensor_tensor(flat[i], mag[:, i, :], neg[:, i, :], ALU.subtract)
                dve.drain().then_inc(w_ready, 1)
                stats_dve(dve)
                with dve.Fori(0, NT // LANES) as n:
                    for i in range(LANES):
                        t = n * LANES + i
                        nc.vector.tensor_scalar(xn[:, i, :], x[:, bass.ds(t + QT, 1), :].rearrange("p a c -> p (a c)"),
                                                mv[:, bass.ds(t, 1), 0], rstd[:, bass.ds(t, 1)],
                                                ALU.subtract, ALU.mult).then_inc(xn_ready, 1)
                    for i in range(LANES):
                        dve.wait_ge(gelu_ready, i + 1)
                        nc.vector.bn_stats(hbn[:, i, :], h[:, i, :])
                        dve.drain()
                        nc.vector.bn_aggr(hmv[:, i, :], hbn[:, i, :])
                        dve.drain()
                        nc.vector.tensor_scalar(hve[:, i:i + 1], hmv[:, i, 1:2], LN_EPS, None, ALU.add)\
                            .then_inc(hve_ready, 1)
                        if i:
                            normalise(dve, i - 1)
                    normalise(dve, LANES - 1)
                    for i in range(LANES):
                        dve.wait_ge(proj_ready, i + 1)
                        at = x[:, bass.ds(n * LANES + i + QT, 1), :].rearrange("p a c -> p (a c)")
                        nc.vector.scalar_tensor_tensor(out=at, in0=pb[i][:, 0:D], scalar=tgate[:, 0:1], in1=at,
                                                       op0=ALU.mult, op1=ALU.add).then_inc(proj_read, 1)
                    for s in (gelu_ready, hrs_ready, proj_ready):
                        dve.sem_inc(s, -LANES)



def expert_ffn(nc, x, stats, ident, d, out):
    TT = 4
    T = TT * P
    NG = NT // TT
    FC = FE // P
    with ExitStack() as ctx:
        def sb(name, shape, dt=F32):
            return ctx.enter_context(nc.sbuf_tensor(f"f1_{name}", shape, dt))

        def pb(name):
            return ctx.enter_context(nc.psum_tensor(f"f1_{name}", [P, 512], F32))

        def sem(name):
            return ctx.enter_context(nc.semaphore(f"f1_{name}"))

        bn, mv, ve, rstd, minus_half = stats
        w1 = sb("w1", [P, NE, FE])
        w3 = sb("w3", [P, NE, FE])
        w2 = sb("w2", [P, NE, FC, D])
        router = sb("router", [P, NE])
        below = sb("below", [P, NE, NE])
        gate = sb("gate", [P, 1])
        tgate = sb("tgate", [P, 1])
        xn = sb("xn", [P, TT, D])
        xnT = sb("xnT", [P, T])
        logits = sb("logits", [P, TT, NE])
        gt = sb("gt", [P, TT, NE, NE])
        eq = sb("eq", [P, TT, NE, NE])
        rank = sb("rank", [P, TT, NE])
        sel = sb("sel", [P, TT, NE])
        picked = sb("picked", [P, TT, NE])
        both = sb("both", [P, TT])
        lead = sb("lead", [P, TT, NE])
        th = sb("th", [P, TT, NE])
        comb = sb("comb", [P, TT, NE])
        sg = sb("sg", [P, 2, T])
        hT = sb("hT", [P, 4, T])
        acc = sb("acc", [P, TT, D])
        res = sb("res", [P, 2, TT, D])
        pt = pb("pt")
        pg = [pb("pg0"), pb("pg1")]
        pu = [pb("pu0"), pb("pu1")]
        po = [pb("po0"), pb("po1")]

        loaded = sem("loaded")
        ve_ready, rstd_ready = sem("ve_ready"), sem("rstd_ready")
        xn_ready = sem("xn_ready")
        xnT_ready = sem("xnT_ready")
        xnT_copied = sem("xnT_copied")
        logits_ready = sem("logits_ready")
        lead_ready = sem("lead_ready")
        th_ready = sem("th_ready")
        gates_ready = sem("gates_ready")
        ups_ready = sem("ups_ready")
        silu_ready = sem("silu_ready")
        hidden_ready = sem("hidden_ready")
        expert_ready = sem("expert_ready")
        expert_read = sem("expert_read")
        res_ready = sem("res_ready")
        stored = [sem("stored0"), sem("stored1")]
        res_free = sem("res_free")
        sg_used = sem("sg_used")
        NC = NE * FC

        with nc.Block() as block:
            stats_dve, stats_pool = layer_norm_stats(nc, block, x, bn, mv, ve, rstd, minus_half,
                                                     ve_ready, rstd_ready)

            @block.sync
            def _(sp):
                sp.dma_start(router[:, :], d["router"]).then_inc(loaded, 16)
                sp.dma_start(below[:, :, :], d["below"].partition_broadcast(P)).then_inc(loaded, 16)
                sp.dma_start(gate[:, :], d["gate"].partition_broadcast(P)).then_inc(loaded, 16)
                sp.dma_start(w1[:, :, :], d["w1"].rearrange("e h f -> h e f")).then_inc(loaded, 16)
                sp.dma_start(w3[:, :, :], d["w3"].rearrange("e h f -> h e f")).then_inc(loaded, 16)
                sp.dma_start(w2[:, :, :, :], d["w2"].rearrange("e (c p) h -> p e c h", p=P)).then_inc(loaded, 16)
                out_v = out.rearrange("b (t p) c -> p (b t) c", p=P)
                with sp.Fori(0, NG // 2) as n:
                    for k in range(2):
                        sp.wait_ge(res_ready, k + 1)
                        sp.dma_start(out_v[:, bass.ds((n * 2 + k) * TT, TT), :], res[:, k]).then_inc(stored[k], 16)
                    for k in range(2):
                        sp.wait_ge(stored[k], 16)
                        sp.sem_inc(stored[k], -16)
                        sp.sem_inc(res_free, 1)
                    sp.sem_inc(res_ready, -2)

            @block.tensor
            def _(pe):
                pe.wait_ge(loaded, 96)
                with pe.Fori(0, NG):
                    pe.wait_ge(xn_ready, 1)
                    for i in range(TT):
                        mm = nc.tensor.transpose(pt[:, i * P:(i + 1) * P], xn[:, i, :], ident[:, :])
                    mm.then_inc(xnT_ready, 1)
                    pe.wait_ge(xnT_copied, 1)
                    for i in range(TT):
                        mm = nc.tensor.matmul(pt[:, i * NE:(i + 1) * NE], xnT[:, i * P:(i + 1) * P], router[:, :],
                                              start=True, stop=True)
                    mm.then_inc(logits_ready, 1)
                    for e in range(NE + 1):
                        for c in range(FC if e < NE else 0):
                            k = e * FC + c
                            if k >= 2:
                                pe.wait_ge(hidden_ready, k - 1)
                            nc.tensor.matmul(pg[k % 2][:, :], w1[:, e, c * P:(c + 1) * P], xnT[:, :],
                                             start=True, stop=True).then_inc(gates_ready, 1)
                            nc.tensor.matmul(pu[k % 2][:, :], w3[:, e, c * P:(c + 1) * P], xnT[:, :],
                                             start=True, stop=True).then_inc(ups_ready, 1)
                        if e > 0:
                            f = e - 1
                            pe.wait_ge(hidden_ready, FC * (f + 1))
                            if f >= 2:
                                pe.wait_ge(expert_read, f - 1)
                            for i in range(TT):
                                for c in range(FC):
                                    mm = nc.tensor.matmul(po[f % 2][:, i * P:(i + 1) * P],
                                                          hT[:, (f * FC + c) % 4, i * P:(i + 1) * P],
                                                          w2[:, f, c, :], start=(c == 0), stop=(c == FC - 1))
                            mm.then_inc(expert_ready, 1)
                    pe.wait_ge(expert_read, NE)
                    pe.sem_inc(xn_ready, -1)
                    pe.sem_inc(xnT_copied, -1)
                    pe.sem_inc(hidden_ready, -NC)
                    pe.sem_inc(expert_read, -NE)

            @block.scalar
            def _(act):
                act.wait_ge(loaded, 96)
                nc.scalar.activation(tgate[:, :], gate[:, :], ACT.Tanh)
                with act.Fori(0, NG):
                    act.wait_ge(xnT_ready, 1)
                    nc.scalar.copy(xnT[:, :], pt[:, :]).then_inc(xnT_copied, 1)
                    for k in range(NC):
                        act.wait_ge(gates_ready, k + 1)
                        if k >= 2:
                            act.wait_ge(sg_used, k - 1)
                        nc.scalar.activation(sg[:, k % 2, :], pg[k % 2][:, :], ACT.Silu).then_inc(silu_ready, 1)
                        if k == 1:
                            act.wait_ge(lead_ready, 1)
                            nc.scalar.activation(th[:, :, :], lead[:, :, :], ACT.Tanh, scale=0.5).then_inc(th_ready, 1)
                    act.wait_ge(sg_used, NC)
                    act.sem_inc(xnT_ready, -1)
                    act.sem_inc(gates_ready, -NC)
                    act.sem_inc(lead_ready, -1)
                    act.sem_inc(sg_used, -NC)

            @block.gpsimd
            def _(pool):
                stats_pool(pool)

            def tiles(dve, n, half):
                for i in range(TT):
                    t = n * TT + i
                    ins = nc.vector.tensor_scalar(xn[:, i, :], x[:, bass.ds(t + QT, 1), :].rearrange("p a c -> p (a c)"),
                                                  mv[:, bass.ds(t, 1), 0], rstd[:, bass.ds(t, 1)],
                                                  ALU.subtract, ALU.mult)
                ins.then_inc(xn_ready, 1)
                dve.wait_ge(logits_ready, 1)
                nc.vector.tensor_copy(logits[:, :, :], pt[:, 0:TT * NE].rearrange("p (t e) -> p t e", e=NE))
                dve.drain()
                mine = logits[:, :, :].unsqueeze(3).broadcast_to([P, TT, NE, NE])
                other = logits[:, :, :].unsqueeze(2).broadcast_to([P, TT, NE, NE])
                nc.vector.tensor_tensor(gt[:], other, mine, ALU.is_gt)
                nc.vector.tensor_tensor(eq[:], other, mine, ALU.is_equal)
                dve.drain()
                nc.vector.tensor_tensor(eq[:], eq[:], below[:, :, :].unsqueeze(1).broadcast_to([P, TT, NE, NE]), ALU.mult)
                dve.drain()
                nc.vector.tensor_tensor(gt[:], gt[:], eq[:], ALU.add)
                dve.drain()
                nc.vector.tensor_reduce(rank[:], gt[:], AX.X, ALU.add)
                dve.drain()
                nc.vector.tensor_scalar(sel[:], rank[:], 2.0, None, ALU.is_lt)
                dve.drain()
                nc.vector.tensor_tensor(picked[:], sel[:], logits[:], ALU.mult)
                dve.drain()
                nc.vector.tensor_reduce(both[:], picked[:], AX.X, ALU.add)
                dve.drain()
                nc.vector.scalar_tensor_tensor(out=lead[:], in0=logits[:], scalar=2.0,
                                               in1=both[:, :].unsqueeze(2).broadcast_to([P, TT, NE]),
                                               op0=ALU.mult, op1=ALU.subtract).then_inc(lead_ready, 1)
                for e in range(NE + 1):
                    for c in range(FC if e < NE else 0):
                        k = e * FC + c
                        dve.wait_ge(silu_ready, k + 1)
                        dve.wait_ge(ups_ready, k + 1)
                        if k == 2:
                            dve.wait_ge(th_ready, 1)
                            nc.vector.tensor_scalar(th[:], th[:], 0.5, 0.5, ALU.mult, ALU.add)
                            dve.drain()
                            nc.vector.tensor_tensor(comb[:], th[:], sel[:], ALU.mult)
                            dve.drain()
                        if k >= 4:
                            pass
                        nc.vector.tensor_tensor(hT[:, k % 4, :], pu[k % 2][:, :], sg[:, k % 2, :], ALU.mult)\
                            .then_inc(hidden_ready, 1)
                        dve.drain().then_inc(sg_used, 1)
                    if e > 0:
                        f = e - 1
                        dve.wait_ge(expert_ready, f + 1)
                        for i in range(TT):
                            src, dst, wt = po[f % 2][:, i * P:(i + 1) * P], acc[:, i, :], comb[:, i, f:f + 1]
                            if f == 0:
                                ins = nc.vector.tensor_scalar(dst, src, wt, None, ALU.mult)
                            else:
                                ins = nc.vector.scalar_tensor_tensor(out=dst, in0=src, scalar=wt, in1=dst,
                                                                     op0=ALU.mult, op1=ALU.add)
                        ins.then_inc(expert_read, 1)
                        dve.drain()
                dve.wait_ge(res_free, half + 1)
                nc.vector.scalar_tensor_tensor(out=res[:, half], in0=acc[:], scalar=tgate[:, 0:1],
                                               in1=x[:, bass.ds(n * TT + QT, TT), :], op0=ALU.mult, op1=ALU.add)\
                    .then_inc(res_ready, 1)
                dve.sem_inc(logits_ready, -1)
                dve.sem_inc(th_ready, -1)
                dve.sem_inc(silu_ready, -NC)
                dve.sem_inc(ups_ready, -NC)
                dve.sem_inc(expert_ready, -NE)

            @block.vector
            def _(dve):
                dve.wait_ge(loaded, 96)
                stats_dve(dve)
                dve.sem_inc(res_free, 2)
                with dve.Fori(0, NG // 2) as n:
                    for half in range(2):
                        tiles(dve, n * 2 + half, half)
                    dve.sem_inc(res_free, -2)


def flamingo(nc, d, out):
    with ExitStack() as ctx:
        def sb(name, shape, dt=F32):
            return ctx.enter_context(nc.sbuf_tensor(name, shape, dt))

        x = sb("x", [P, NT + QT, D])
        stats = (sb("bn", [P, NT, 6]), sb("mv", [P, NT, 2]), sb("ve", [P, NT]), sb("rstd", [P, NT]),
                 sb("minus_half", [P, NT]))
        ident = sb("ident", [P, P])
        ident_bf = sb("ident_bf", [P, P], BF16)
        head_of = sb("head_of", [P, 2])
        row_of = sb("row_of", [6, 2])
        kscr = nc.dram_tensor("key_parts", [2, 3, HP, 2 * DH, S2], BF16, kind="Internal").ap()
        qscr = nc.dram_tensor("query_parts", [2, 4, HP, 2 * DH, 2 * S], BF16, kind="Internal").ap()
        bscr = nc.dram_tensor("key_bias", [B + 1, S2P], BF16, kind="Internal").ap()
        keepscr = nc.dram_tensor("key_mask", [B, S2], BF16, kind="Internal").ap()
        consts_in = ctx.enter_context(nc.semaphore("consts_in"))

        with nc.Block() as block:
            @block.sync
            def _(sp):
                sp.dma_start(ident[:, :], d["ident"]).then_inc(consts_in, 16)
                sp.dma_start(head_of[:, :], d["head_of"]).then_inc(consts_in, 16)
                sp.dma_start(row_of[:, :], d["row_of"]).then_inc(consts_in, 16)
                sp.wait_ge(consts_in, 48)

            @block.vector
            def _(dve):
                nc.vector.memset(x[:, 0:QT, :], 0.0)
                dve.wait_ge(consts_in, 48)
                nc.vector.tensor_copy(ident_bf[:, :], ident[:, :])

        scratch = (kscr, qscr, bscr, keepscr)
        attention(nc, 0, x, stats, ident, ident_bf, head_of, row_of, {
            "x": d["x"], "keep": d["keep"], "ctxT": d["ctxT"], "gate": d["g_xattn"][0:1],
            "wq": d["wq0"], "wk": d["wk0"], "wv": d["wv0"], "wo": d["wo0"],
            "bq": d["bq0"], "bk": d["bk0"], "bv": d["bv0"], "bo": d["bo0"]}, scratch)
        ternary_ffn(nc, x, stats, ident, {
            "w_fcT": d["w_fcT"], "w_projT": d["w_projT"], "ln_w": d["ln_w"], "ln_b": d["ln_b"],
            "gate": d["g_ffn"][0:1]})
        attention(nc, 1, x, stats, ident, ident_bf, head_of, row_of, {
            "mask": d["mask"], "ctxT": d["ctxT"], "gate": d["g_xattn"][1:2],
            "wq": d["wq1"], "wk": d["wk1"], "wv": d["wv1"], "wo": d["wo1"], "bo": d["bo1"]}, scratch)
        expert_ffn(nc, x, stats, ident, {
            "router": d["router"], "below": d["below"], "w1": d["w1"], "w3": d["w3"], "w2": d["w2"],
            "gate": d["g_ffn"][1:2]}, out)


def kernel(**inputs):
    import numpy as np
    import concourse.bacc as bacc
    from concourse.bass_utils import run_bass_kernel_spmd

    a = {k: np.asarray(v) for k, v in inputs.items()}
    rows = np.arange(P)
    layout = {
        "x": a["x"],
        "ctxT": a["ctx_1024"].transpose(0, 2, 1),
        "keep": a["mask_BxS2_bf1"].view(np.uint8),
        "mask": a["mask_Bx1xSxS2_ik1"][:, 0],
        "g_xattn": a["g_xattn"], "g_ffn": a["g_ffn"],
        "wq0": a["L0_xattn_Wq"].T, "wk0": a["L0_xattn_Wk"].T, "wv0": a["L0_xattn_Wv"].T, "wo0": a["L0_xattn_Wo"].T,
        "bq0": a["L0_xattn_bq"].reshape(P, 1), "bk0": a["L0_xattn_bk"].reshape(P, 1),
        "bv0": a["L0_xattn_bv"], "bo0": a["L0_xattn_bo"],
        "w_fcT": a["L0_ffn_W_fc"].T, "w_projT": a["L0_ffn_W_proj"].T,
        "ln_w": a["L0_ffn_ln_w"].reshape(FF // P, P).T, "ln_b": a["L0_ffn_ln_b"].reshape(FF // P, P).T,
        "wq1": a["L1_xattn_Wq"].T, "wk1": a["L1_xattn_Wk"].T, "wv1": a["L1_xattn_Wv"].T, "wo1": a["L1_xattn_Wo"].T,
        "bo1": a["L1_xattn_bo"],
        "router": a["L1_ffn_router_w"], "w1": a["L1_ffn_w1"], "w3": a["L1_ffn_w3"], "w2": a["L1_ffn_w2"],
        "ident": np.eye(P, dtype=np.float32),
        "head_of": (rows[:, None] // DH % 2 == np.arange(2)).astype(np.float32),
        "row_of": (np.arange(6)[:, None] // 3 == np.arange(2)).astype(np.float32),
        "below": np.tril(np.ones((NE, NE), np.float32), -1),
    }
    nc = bacc.Bacc("TRN2", target_bir_lowering=False, num_devices=1)
    arrays, d = {}, {}
    for name, v in layout.items():
        v = np.ascontiguousarray(v)
        arrays[f"in_{name}"] = v
        d[name] = nc.dram_tensor(f"in_{name}", v.shape, mybir.dt.from_np(v.dtype), kind="ExternalInput").ap()
    out = nc.dram_tensor("out_x", (B, S, D), F32, kind="ExternalOutput").ap()
    flamingo(nc, d, out)
    r = run_bass_kernel_spmd(nc, [arrays], core_ids=[0])
    return r.results[0]["out_x"]
```

```python
from contextlib import ExitStack

import concourse.bass as bass
from concourse import mybir
from concourse.alu_op_type import AluOpType as ALU

B, S, D = 16, 256, 128
S2 = 1601
H, DH = 16, 8
P = 128
QT = S // P
KT = -(-S2 // P)
S2P = KT * P
NT = B * QT
FF = 512
NE, FE = 8, 256
HP = H // 2

K_PARTS = (0, 1, 0, 1, 2, 0)
Q_PARTS = (0, 0, 1, 1, 0, 2)
NPROD = len(K_PARTS)
ROWS_OF_HEADS = 2 * DH
MAX_ROW = NPROD * ROWS_OF_HEADS
BIAS_ROW = MAX_ROW + 6

SCALE = float(DH) ** -0.5
LN_EPS = 1e-5
GAMMA_EPS = 1e-6
MASKED = -(2.0 ** 100)
PADDED = -(2.0 ** 120)

F32 = mybir.dt.float32
BF16 = mybir.dt.bfloat16
I32 = mybir.dt.int32
U8 = mybir.dt.uint8
ACT = mybir.ActivationFunctionType
AX = mybir.AxisListType

GROUPS = HP // 2
UNITS = GROUPS * KT * 2
HALF = UNITS // 2
KW = (401, 400, 400, 400)
KO = (0, 401, 801, 1201)
CHUNKS = HP * 2 * QT * 4
LAG = 3
NSB = 3
NPB = 4
NRB = 2


def chunks_at(u, after=None):
    return [n for n in range(CHUNKS) if n * 203 // CHUNKS // 2 == u
            and after in (None, n * 203 // CHUNKS % 2)]


def unit(u):
    g, r = divmod(u, 2 * KT)
    return g, r // 2, 2 * g + r % 2, r % 2


AT_EPI = (6, 9)
AT_MAX_B = 12
AT_EPI_T = 18
AT_EPI_W = 21
AT_NORM = (13, 15)
AT_XN = 25
AT_Q = 28
AT_KP = (31, 34, 37, 40)
AT_MAX_A = 56
AT_V = (66, 69, 72, 75)
AT_MASK = (78, 82, 86, 90)
SPLIT = 5
HALF_MAX = 50
assert all(n >= CHUNKS // 2 for u in range(HALF_MAX + 1, UNITS) for n in chunks_at(u))
AT_Q_HI, AT_Q_MID = 30, 36
AT_K_HI, AT_K_MID = 47, 60
VT = ((0, 4), (4, 8), (8, 12), (12, 13))


def layer_norm_stats(nc, block, x, bn, mv, ve, rstd, minus_half, ve_ready, rstd_ready, x_in=None):

    def on_vector(dve):
        if x_in is not None:
            dve.wait_ge(x_in, 16)
        for t in range(NT):
            nc.vector.bn_stats(bn[:, t, :], x[:, QT + t, :])
        dve.drain()
        for t in range(NT):
            nc.vector.bn_aggr(mv[:, t, :], bn[:, t, :])
        dve.drain()
        nc.vector.tensor_scalar(ve[:], mv[:, :, 1], LN_EPS, None, ALU.add).then_inc(ve_ready, 1)

    def on_gpsimd(pool):
        nc.gpsimd.memset(minus_half[:], -0.5)
        pool.drain()
        pool.wait_ge(ve_ready, 1)
        nc.gpsimd.tensor_tensor(rstd[:], ve[:], minus_half[:], ALU.pow).then_inc(rstd_ready, 1)

    return on_vector, on_gpsimd


def attention(nc, layer, x, stats, ident, ident_bf, head_of, row_of, d, scratch, kept):
    first = layer == 0
    with ExitStack() as ctx:
        def sb(name, shape, dt):
            return ctx.enter_context(nc.sbuf_tensor(f"a{layer}_{name}", shape, dt))

        def pb(name, shape, dt=F32):
            return ctx.enter_context(nc.psum_tensor(f"a{layer}_{name}", shape, dt))

        def sem(name):
            return ctx.enter_context(nc.semaphore(f"a{layer}_{name}"))

        bn, mv, ve, rstd, minus_half = stats
        kx, qx, vx, probs, outT = kept
        ctxT = sb("ctxT", [P, 2, S2], F32)
        kf = sb("kf", [P, S2], F32)
        kr = sb("kr", [P, S2], F32)
        kparts = sb("kparts", [P, 3, S2], BF16)
        qf = sb("qf", [P, 2, S], F32)
        qr = sb("qr", [P, 2, S], F32)
        qparts = sb("qparts", [P, 3, 2, S], BF16)
        attn = sb("attn", [P, QT, D], F32)
        attnT = sb("attnT", [P, S], F32)
        rsum = sb("rsum", [P, QT, H], F32)
        step = sb("step", [P, QT, D], F32)
        xn = sb("xn", [P, QT, D], F32)
        xnT = sb("xnT", [P, S], F32)
        mx = sb("mx", [P, QT, HP, 2, 4], F32)
        nm = sb("nm", [P, QT, HP // 2, 2], F32)
        nr = sb("nr", [P, QT, HP // 2, 2], F32)
        nparts = sb("nparts", [P, QT, HP // 2, 2, 3], BF16)
        wq = sb("wq", [P, D], F32)
        wk = sb("wk", [P, D], F32)
        wv = sb("wv", [P, D], F32)
        wo = sb("wo", [P, D], F32)
        bo = sb("bo", [P, D], F32)
        gate = sb("gate", [P, 1], F32)
        tgate = sb("tgate", [P, 1], F32)
        bk = sb("bk", [P, 1], F32)
        bq = sb("bq", [P, 1], F32)
        bq2 = sb("bq2", [P, 2], F32)
        if first:
            bv = sb("bv", [P, D], F32)
            keep = sb("keep", [P, S2], BF16)
            all_keep = sb("all_keep", [B, S2], U8)
            ones_kept = sb("ones_kept", [B, S2], BF16)
            bias = sb("bias", [B + 1, S2P], BF16)
        else:
            mask_in = sb("mask_in", [P, QT, S2], I32)
            mbias = sb("mbias", [P, 2, QT, S2], BF16)
            mbiasT = sb("mbiasT", [P, 2, KT, S], BF16)
            masked = sb("masked", [P, 2, KW[0]], BF16)

        rowmax = [pb(f"rowmax{i}", [P, 512]) for i in range(NRB)]
        scores = [pb(f"scores{i}", [P, 512]) for i in range(NSB)]
        pv = [pb(f"pv{i}", [P, 512]) for i in range(2)]
        shared = pb("shared", [P, 512])
        shared_bf = shared[:, :].bitcast(BF16)

        loaded = sem("loaded")
        x_in = sem("x_in")
        zeroed = sem("zeroed")
        zeros_kept = sem("zeros_kept")
        kx_ready = sem("kx_ready")
        bias_ready = sem("bias_ready")
        ready = sem("ready")
        ve_ready, rstd_ready = sem("ve_ready"), sem("rstd_ready")
        scores_ready = sem("scores_ready")
        probs_ready = sem("probs_ready")
        probs_used = sem("probs_used")
        tail_ready = sem("tail_ready")
        tail_used = sem("tail_used")
        rowmax_ready = sem("rowmax_ready")
        rowmax_read = sem("rowmax_read")
        shared_act = sem("shared_act")
        shared_dve = sem("shared_dve")
        shared_read = sem("shared_read")
        group_copied = sem("group_copied")
        half_done = sem("half_done")
        parts_in = [sem("parts_in0"), sem("parts_in1")]
        ctx_in = [sem("ctx_in0"), sem("ctx_in1")]
        mask_landed = sem("mask_landed")
        mbias_ready = sem("mbias_ready")
        mbias_free = sem("mbias_free")
        kf_ready = sem("kf_ready")
        km_ready = sem("km_ready")
        khi_ready = sem("khi_ready")
        kr_ready = sem("kr_ready")
        kmid_ready = sem("kmid_ready")
        ksplit = sem("ksplit")
        qhi_ready = sem("qhi_ready")
        qr_ready = sem("qr_ready")
        qmid_ready = sem("qmid_ready")
        qsplit = sem("qsplit")
        staged = sem("staged")
        parts_free = sem("parts_free")
        xn_ready = sem("xn_ready")
        step_ready = sem("step_ready")
        step_added = sem("step_added")
        attn_ready = sem("attn_ready")
        nparts_ready = sem("nparts_ready")

        kscr, qscr, bscr, keepscr = scratch
        NPARTS_DMA = 16 * (2 * NPROD + 2)

        with nc.Block() as block:
            stats_dve, stats_pool = layer_norm_stats(nc, block, x, bn, mv, ve, rstd, minus_half,
                                                     ve_ready, rstd_ready, x_in if first else None)

            @block.sync
            def _(sp):
                n = 0
                if first:
                    sp.dma_start(x[:, QT:, :], d["x"].rearrange("b (t p) c -> p (b t) c", p=P)).then_inc(x_in, 16)
                    sp.dma_start(all_keep[:, :], d["keep"]).then_inc(loaded, 16)
                    sp.dma_start(bv[:, :], d["bv"].partition_broadcast(P)).then_inc(loaded, 16)
                    sp.dma_start(bq[:, :], d["bq"]).then_inc(loaded, 16)
                    sp.dma_start(bk[:, :], d["bk"]).then_inc(loaded, 16)
                    n = 4
                for w, name in ((wq, "wq"), (wk, "wk"), (wv, "wv"), (wo, "wo")):
                    sp.dma_start(w[:, :], d[name]).then_inc(loaded, 16)
                sp.dma_start(bo[:, :], d["bo"].partition_broadcast(P)).then_inc(loaded, 16)
                sp.dma_start(gate[:, :], d["gate"].partition_broadcast(P)).then_inc(loaded, 16)
                sp.wait_ge(loaded, 16 * (n + 6))
                if first:
                    sp.wait_ge(zeroed, 1)
                    for par in range(2):
                        sp.dma_start(qscr[par, 3].rearrange("p c q -> (p c) q"),
                                     qparts[:, 0].rearrange("p j q -> p (j q)")).then_inc(zeros_kept, 16)
                    sp.wait_ge(bias_ready, 1)
                    sp.dma_start(bscr, bias[:, :]).then_inc(zeros_kept, 16)
                    sp.dma_start(keepscr, ones_kept[:, :]).then_inc(zeros_kept, 16)
                    sp.wait_ge(zeros_kept, 64)

            @block.vector
            def _(dve):
                if first:
                    nc.vector.memset(qparts[:], 0.0).then_inc(zeroed, 1)
                    stats_dve(dve)
                    nc.vector.memset(probs[:], 1.0)
                    nc.vector.memset(outT[:], 1.0)
                nc.vector.memset(pv[0][:], 0.0)
                nc.vector.memset(pv[1][:], 0.0)
                if first:
                    nc.vector.memset(bias[:], 0.0)
                    dve.drain()
                    nc.vector.memset(bias[:, S2:S2P], PADDED)
                    dve.wait_ge(loaded, 16 * 10)
                    nc.vector.tensor_copy(ones_kept[:, :], all_keep[:, :])
                    nc.vector.tensor_scalar(bias[0:B, 0:S2], all_keep[:, :], -1.0, -MASKED,
                                            ALU.add, ALU.mult)
                    dve.drain()
                    nc.vector.tensor_scalar(bq2[:, :], head_of[:, :], bq[:, 0:1], None, ALU.mult)\
                        .then_inc(bias_ready, 1)
                else:
                    nc.vector.memset(bk[:], 0.0)
                    nc.vector.memset(bq2[:], 0.0)
                    stats_dve(dve)
                dve.wait_ge(rstd_ready, 1)

            @block.scalar
            def _(act):
                act.wait_ge(loaded, 16 * (10 if first else 6))
                nc.scalar.activation(tgate[:, :], gate[:, :], ACT.Tanh)

            @block.gpsimd
            def _(pool):
                if first:
                    nc.gpsimd.memset(qx[:], 0.0)
                    nc.gpsimd.memset(vx[:], 0.0)
                    pool.drain()
                    nc.gpsimd.memset(vx[:, :, 0:KT - 1, :, DH:DH + 1], 1.0)
                    pool.drain()
                    nc.gpsimd.memset(vx[0:S2 - (KT - 1) * P, :, KT - 1, :, DH:DH + 1], 1.0)
                    pool.drain()
                    nc.gpsimd.memset(qx[MAX_ROW:BIAS_ROW + 1], 1.0)
                    pool.drain()
                else:
                    nc.gpsimd.memset(mbiasT[:, :, KT - 1, :], 0.0)
                    pool.drain()
                stats_pool(pool)


        def pe_body(par, exp, mx_on, prep, vals, epi):
            nxt = 1 - par
            rounds = [0]

            def shared_free():
                if rounds[0]:
                    pe.wait_ge(shared_read, rounds[0])
                rounds[0] += 1

            def qk(u):
                g, t, p, _ = unit(u)
                out = scores[u % NSB][:, :]
                mm = nc.tensor.matmul(out, kx[:, par, p, t * P:(t + 1) * P], qx[:, par, p, :, :],
                                      start=True, stop=first)
                if not first:
                    mm = nc.tensor.matmul(out, ident_bf[:, :],
                                          mbiasT[:, par, t:t + 1, :].broadcast_to([P, 2, S]),
                                          start=False, stop=True)
                mm.then_inc(scores_ready, 1)

            def values(u, of=par):
                g, t, p, a = unit(u)
                if t == 0 and a == 0:
                    if g == 0:
                        pe.wait_ge(group_copied, GROUPS - 1)
                    if g >= 2:
                        pe.wait_ge(group_copied, g - 1)
                for j in range(2):
                    row = 32 * (2 * a + j)
                    mm = nc.tensor.matmul(pv[g % 2][row:row + DH + 1, 0:S], vx[:, of, t, 2 * p + j, :],
                                          probs[:, u % NPB, j * S:(j + 1) * S],
                                          start=(t == 0), stop=(t == KT - 1), skip_group_check=True)
                    if j == 0 and u in (HALF - LAG + 1, UNITS - LAG - 1):
                        mm.then_inc(half_done, 1)
                mm.then_inc(probs_used if u < UNITS - LAG else tail_used, 1)

            def chunk(n):
                p, j, qt, c = n // 16, n // 8 % 2, n // 4 % 2, n % 4
                if n == 0:
                    pe.wait_ge(parts_in[0], NPARTS_DMA)
                    pe.sem_inc(parts_in[0], -NPARTS_DMA)
                if n == CHUNKS // 2:
                    pe.wait_ge(parts_in[1], NPARTS_DMA)
                    pe.sem_inc(parts_in[1], -NPARTS_DMA)
                if n >= NRB:
                    pe.wait_ge(rowmax_read, n - NRB + 1)
                nc.tensor.matmul(rowmax[n % NRB][:, 0:KW[c]], qx[:, nxt, p, j, qt * P:(qt + 1) * P],
                                 kx[:, nxt, p, KO[c]:KO[c] + KW[c]], start=True, stop=True)\
                    .then_inc(rowmax_ready, 1)
                if not exp and n in (1, CHUNKS // 2 + 1):
                    pe.drain().then_inc(half_done, 1)

            def put_maxima(par_of, half, waits):
                pe.wait_ge(nparts_ready, waits)
                shared_free()
                for p in range(HP // 2):
                    for qt in range(QT):
                        o = (p * QT + qt) * P
                        mm = nc.tensor.transpose(shared_bf[0:6, o:o + P],
                                                 nparts[:, qt, p, :, :], ident_bf[:, :])
                mm.then_inc(shared_act, 1)

            nmax = [0]
            for u in range(UNITS):
                if epi and u < LAG:
                    pe.wait_ge(tail_ready, min(u + 2, LAG))
                    if u == LAG - 1:
                        pe.sem_inc(tail_ready, -LAG)
                if exp and u >= LAG:
                    pe.wait_ge(probs_ready, u - LAG + 1)
                if exp:
                    qk(u)
                if mx_on:
                    for n in chunks_at(u, 0):
                        chunk(n)
                if epi and u < LAG:
                    values(UNITS - LAG + u, nxt)
                if exp and u >= LAG:
                    values(u - LAG)
                if mx_on:
                    for n in chunks_at(u, 1):
                        chunk(n)
                if epi and u == AT_EPI[0]:
                    pe.wait_ge(group_copied, GROUPS)
                    pe.sem_inc(group_copied, -GROUPS)
                if epi and u in AT_EPI:
                    qt = AT_EPI.index(u)
                    shared_free()
                    for g in range(GROUPS):
                        mm = nc.tensor.transpose(shared[:, g * P:(g + 1) * P],
                                                 outT[:, g, qt * P:(qt + 1) * P], ident[:, :])
                    mm.then_inc(shared_dve, 1)
                if exp and u == AT_MAX_B:
                    nmax[0] += 1
                    put_maxima(par, 1, nmax[0])
                if epi and u == AT_EPI_T:
                    pe.wait_ge(attn_ready, 1)
                    shared_free()
                    for qt in range(QT):
                        mm = nc.tensor.transpose(shared[:, qt * P:(qt + 1) * P], attn[:, qt, :], ident[:, :])
                    mm.then_inc(shared_act, 1)
                if epi and u == AT_EPI_W:
                    shared_free()
                    for qt in range(QT):
                        mm = nc.tensor.matmul(shared[:, qt * P:(qt + 1) * P],
                                              attnT[:, qt * P:(qt + 1) * P], wo[:, :], start=True, stop=True)
                    mm.then_inc(shared_dve, 1)
                if prep and u == AT_XN:
                    pe.wait_ge(xn_ready, 1)
                    shared_free()
                    for qt in range(QT):
                        mm = nc.tensor.transpose(shared[:, qt * P:(qt + 1) * P], xn[:, qt, :], ident[:, :])
                    mm.then_inc(shared_act, 1)
                if prep and u == AT_Q:
                    shared_free()
                    nc.tensor.matmul(shared[:, 0:S], wq[:, :], xnT[:, :], start=True, stop=True)\
                        .then_inc(shared_act, 1)
                if prep and u in AT_KP:
                    i = AT_KP.index(u)
                    if i == 0:
                        pe.wait_ge(ctx_in[par], 16)
                        pe.sem_inc(ctx_in[par], -16)
                    shared_free()
                    nc.tensor.matmul(shared[:, 0:KW[i]], wk[:, :], ctxT[:, par, KO[i]:KO[i] + KW[i]],
                                     start=True, stop=True).then_inc(shared_act, 1)
                if mx_on and u == AT_MAX_A:
                    nmax[0] += 1
                    put_maxima(nxt, 0, nmax[0])
                if vals and u in AT_V:
                    shared_free()
                    for t in range(*VT[AT_V.index(u)]):
                        w = min(P, S2 - t * P)
                        o = t % 4 * P
                        mm = nc.tensor.matmul(shared[0:w, o:o + D], ctxT[:, nxt, t * P:t * P + w],
                                              wv[:, :], start=True, stop=True)
                    mm.then_inc(shared_act, 1)
                if vals and not first and u in AT_MASK:
                    shared_free()
                    for t in range(*VT[AT_MASK.index(u)]):
                        w = min(P, S2 - t * P)
                        for qt in range(QT):
                            o = (t % 4 * QT + qt) * P
                            mm = nc.tensor.transpose(shared_bf[0:w, o:o + P],
                                                     mbias[:, nxt, qt, t * P:t * P + w], ident_bf[:, :])
                    mm.then_inc(shared_act, 1)
            if mx_on and not exp:
                pe.drain().then_inc(half_done, 1)
            if exp:
                pe.sem_inc(probs_ready, -(UNITS - LAG))
            if mx_on:
                pe.wait_ge(rowmax_read, CHUNKS)
                pe.sem_inc(rowmax_read, -CHUNKS)
            if rounds[0]:
                pe.wait_ge(shared_read, rounds[0])
                pe.sem_inc(shared_read, -rounds[0])
            if nmax[0]:
                pe.sem_inc(nparts_ready, -nmax[0])
            if epi:
                pe.sem_inc(attn_ready, -1)
            if prep:
                pe.sem_inc(xn_ready, -1)

        def act_body(par, exp, mx_on, prep, vals, epi):
            nxt = 1 - par
            rounds = [0]

            def shared_full():
                rounds[0] += 1
                act.wait_ge(shared_act, rounds[0])

            def put_maxima(par_of, half, i):
                if i == 0:
                    shared_full()
                j, pp = i // 2, i % 2
                ins = nc.scalar.activation(
                    qx[MAX_ROW:BIAS_ROW, par_of, 4 * half + 2 * pp:4 * half + 2 * pp + 2, j, :],
                    shared_bf[0:6, 512 * pp:512 * (pp + 1)].rearrange("r (p q) -> r p q", q=S), ACT.Copy,
                    scale=row_of[0:6, j:j + 1])
                if i == 3:
                    ins.then_inc(shared_read, 1)

            def group(g):
                if g < GROUPS - 1:
                    act.wait_ge(probs_used, 2 * KT * (g + 1))
                else:
                    act.wait_ge(tail_used, LAG)
                    act.sem_inc(tail_used, -LAG)
                nc.scalar.copy(outT[:, g, :], pv[g % 2][:, 0:S]).then_inc(group_copied, 1)

            if epi:
                act.wait_ge(probs_used, UNITS - LAG)
                act.sem_inc(probs_used, -(UNITS - LAG))
            for u in range(UNITS):
                if exp:
                    act.wait_ge(scores_ready, u + 1)
                    if u >= NPB:
                        act.wait_ge(probs_used, u - NPB + 1)
                    elif epi and u:
                        act.wait_ge(tail_used, u)
                    nc.scalar.activation(probs[:, u % NPB, :], scores[u % NSB][:, :], ACT.Exp, scale=SCALE)\
                        .then_inc(probs_ready if u < UNITS - LAG else tail_ready, 1)
                if epi and u == NPB - 1:
                    group(GROUPS - 1)
                if exp and u > LAG + 1 and (u - LAG - 1) % (2 * KT) == 2 * KT - 1:
                    group((u - LAG - 1) // (2 * KT))
                if exp and AT_MAX_B <= u < AT_MAX_B + 4:
                    put_maxima(par, 1, u - AT_MAX_B)
                if epi and u == AT_EPI_T:
                    shared_full()
                    nc.scalar.copy(attnT[:, :], shared[:, 0:S]).then_inc(shared_read, 1)
                if prep and u == AT_XN:
                    shared_full()
                    nc.scalar.copy(xnT[:, :], shared[:, 0:S]).then_inc(shared_read, 1)
                if prep and u == AT_Q:
                    shared_full()
                    for j in range(2):
                        ins = nc.scalar.activation(qf[:, j, :], shared[:, 0:S], ACT.Identity,
                                                   scale=head_of[:, j:j + 1], bias=bq2[:, j:j + 1])
                    ins.then_inc(shared_read, 1)
                if prep and u == AT_Q_HI:
                    act.wait_ge(parts_free, 1)
                    act.sem_inc(parts_free, -1)
                    act.drain()
                    nc.scalar.copy(qparts[:, 0], qf[:, :, :]).then_inc(qhi_ready, 1)
                if prep and u == AT_Q_MID:
                    act.wait_ge(qr_ready, 1)
                    act.sem_inc(qr_ready, -1)
                    nc.scalar.copy(qparts[:, 1], qr[:, :, :]).then_inc(qmid_ready, 1)
                if prep and u in AT_KP:
                    i = AT_KP.index(u)
                    shared_full()
                    nc.scalar.activation(kf[:, KO[i]:KO[i] + KW[i]], shared[:, 0:KW[i]], ACT.Identity,
                                         bias=bk[:, 0:1]).then_inc(shared_read, 1)
                    if i == 3:
                        act.drain().then_inc(kf_ready, 1)
                if prep and AT_K_HI <= u < AT_K_HI + 4:
                    i = u - AT_K_HI
                    if first and i == 0:
                        act.wait_ge(km_ready, 1)
                        act.sem_inc(km_ready, -1)
                    ins = nc.scalar.copy(kparts[:, 0, KO[i]:KO[i] + KW[i]], kf[:, KO[i]:KO[i] + KW[i]])
                    if i == 3:
                        ins.then_inc(khi_ready, 1)
                if prep and AT_K_MID <= u < AT_K_MID + 4:
                    i = u - AT_K_MID
                    if i == 0:
                        act.wait_ge(kr_ready, 1)
                        act.sem_inc(kr_ready, -1)
                    ins = nc.scalar.copy(kparts[:, 1, KO[i]:KO[i] + KW[i]], kr[:, KO[i]:KO[i] + KW[i]])
                    if i == 3:
                        ins.then_inc(kmid_ready, 1)
                if mx_on and AT_MAX_A <= u < AT_MAX_A + 4:
                    put_maxima(nxt, 0, u - AT_MAX_A)
                if vals and u in AT_V:
                    a, b = VT[AT_V.index(u)]
                    w = min(P, S2 - a * P)
                    shared_full()
                    nc.scalar.copy(vx[0:w, nxt, a:b, :, 0:DH],
                                   shared[0:w, 0:(b - a) * D].rearrange("k (t h e) -> k t h e", h=H, e=DH))\
                        .then_inc(shared_read, 1)
                if vals and not first and u in AT_MASK:
                    a, b = VT[AT_MASK.index(u)]
                    w = min(P, S2 - a * P)
                    shared_full()
                    nc.scalar.copy(mbiasT[0:w, nxt, a:b, :],
                                   shared_bf[0:w, 0:(b - a) * S].rearrange("k (t q) -> k t q", q=S))\
                        .then_inc(shared_read, 1)
            if exp:
                act.sem_inc(scores_ready, -UNITS)
            if rounds[0]:
                act.sem_inc(shared_act, -rounds[0])

        def dve_body(par, exp, mx_on, prep, vals, epi, b):
            nxt = 1 - par
            rounds = [0]

            def shared_full():
                rounds[0] += 1
                dve.wait_ge(shared_dve, rounds[0])

            def split_maxima(half, i):
                dve.drain()
                if i == 0:
                    nc.vector.tensor_reduce(nm[:], mx[:, :, 4 * half:4 * half + 4, :, :], AX.X, ALU.max, negate=True)
                elif i == 1:
                    nc.vector.tensor_copy(nparts[:, :, :, :, 0], nm[:])
                elif i == 2:
                    nc.vector.tensor_tensor(nr[:], nm[:], nparts[:, :, :, :, 0], ALU.subtract)
                elif i == 3:
                    nc.vector.tensor_copy(nparts[:, :, :, :, 1], nr[:])
                else:
                    nc.vector.tensor_tensor(nparts[:, :, :, :, 2], nr[:], nparts[:, :, :, :, 1], ALU.subtract)\
                        .then_inc(nparts_ready, 1)

            for u in range(UNITS):
                if mx_on:
                    for n in chunks_at(u):
                        p, j, qt, c = n // 16, n // 8 % 2, n // 4 % 2, n % 4
                        dve.wait_ge(rowmax_ready, n + 1)
                        src, dst = rowmax[n % NRB][:, 0:KW[c]], mx[:, qt, p, j, c:c + 1]
                        if first:
                            nc.vector.tensor_reduce(dst, src, AX.X, ALU.max).then_inc(rowmax_read, 1)
                        else:
                            if n == 0:
                                dve.wait_ge(mbias_ready, 1)
                                dve.sem_inc(mbias_ready, -1)
                            nc.vector.tensor_tensor_reduce(masked[:, n % 2, 0:KW[c]], src,
                                                           mbias[:, nxt, qt, KO[c]:KO[c] + KW[c]], 1.0, PADDED, ALU.add, ALU.max, dst)\
                                .then_inc(rowmax_read, 1)
                if mx_on and HALF_MAX <= u < HALF_MAX + SPLIT:
                    split_maxima(0, u - HALF_MAX)
                if exp and u < SPLIT:
                    split_maxima(1, u)
                if epi and u in AT_EPI:
                    qt = AT_EPI.index(u)
                    shared_full()
                    full = shared[:, :].rearrange("q (h e) -> q h e", e=32)
                    nc.vector.reciprocal(rsum[:, qt, :], full[:, :, DH])
                    dve.drain()
                    o = attn[:, qt, :].rearrange("q (h e) -> q h e", e=DH)
                    ins = nc.vector.tensor_tensor(o, full[:, :, 0:DH],
                                                  rsum[:, qt, :].unsqueeze(2).broadcast_to([P, H, DH]), ALU.mult)
                    ins.then_inc(shared_read, 1)
                    dve.drain()
                    if first:
                        ins = nc.vector.tensor_tensor(attn[:, qt, :], attn[:, qt, :], bv[:, :], ALU.add)
                        if qt == 1:
                            ins.then_inc(attn_ready, 1)
                    elif qt == 1:
                        dve.drain().then_inc(attn_ready, 1)
                if epi and u == AT_EPI_W:
                    dve.wait_ge(step_added, 1)
                    dve.sem_inc(step_added, -1)
                    shared_full()
                    nc.vector.tensor_tensor(step[:], shared[:, 0:S].rearrange("q (t c) -> q t c", t=QT),
                                            bo[:, :].unsqueeze(1).broadcast_to([P, QT, D]), ALU.add)\
                        .then_inc(shared_read, 1)
                    dve.drain().then_inc(step_ready, 1)
                if prep and u in AT_NORM:
                    qt = AT_NORM.index(u)
                    ins = nc.vector.tensor_scalar(xn[:, qt, :],
                                                  x[:, bass.ds((b + 3) * QT + qt, 1), :].rearrange("p a c -> p (a c)"),
                                                  mv[:, bass.ds((b + 2) * QT + qt, 1), 0],
                                                  rstd[:, bass.ds((b + 2) * QT + qt, 1)],
                                                  ALU.subtract, ALU.mult)
                    if qt == QT - 1:
                        ins.then_inc(xn_ready, 1)
            if rounds[0]:
                dve.sem_inc(shared_dve, -rounds[0])
            if mx_on:
                dve.sem_inc(rowmax_ready, -CHUNKS)
                if not first:
                    dve.drain().then_inc(mbias_free, 1)

        def pool_body(par, exp, mx_on, prep, vals, epi, b):
            def residual():
                pool.wait_ge(step_ready, 1)
                pool.sem_inc(step_ready, -1)
                at = x[:, bass.ds(b * QT, QT), :]
                nc.gpsimd.tensor_scalar(step[:], step[:], tgate[:, 0:1], None, ALU.mult)
                pool.drain()
                nc.gpsimd.tensor_tensor(at, at, step[:], ALU.add).then_inc(step_added, 1)

            if not prep:
                if epi:
                    residual()
                return
            if not first:
                pool.wait_ge(mask_landed, 16)
                pool.sem_inc(mask_landed, -16)
                pool.wait_ge(mbias_free, 1)
                pool.sem_inc(mbias_free, -1)
                for qt in range(QT):
                    ins = nc.gpsimd.tensor_scalar(mbias[:, par, qt, :], mask_in[:, qt, :], 0.0, MASKED,
                                                  ALU.is_equal, ALU.mult)
                ins.then_inc(mbias_ready, 1)
            if epi:
                residual()
            pool.wait_ge(qhi_ready, 1)
            pool.sem_inc(qhi_ready, -1)
            nc.gpsimd.tensor_tensor(qr[:, :, :], qf[:, :, :], qparts[:, 0], ALU.subtract).then_inc(qr_ready, 1)
            pool.wait_ge(qmid_ready, 1)
            pool.sem_inc(qmid_ready, -1)
            nc.gpsimd.tensor_tensor(qparts[:, 2], qr[:, :, :], qparts[:, 1], ALU.subtract).then_inc(qsplit, 1)
            pool.wait_ge(kf_ready, 1)
            pool.sem_inc(kf_ready, -1)
            if first:
                pool.wait_ge(mask_landed, 16)
                pool.sem_inc(mask_landed, -16)
                nc.gpsimd.tensor_tensor(kf[:, :], kf[:, :], keep[:, :], ALU.mult).then_inc(km_ready, 1)
            pool.wait_ge(khi_ready, 1)
            pool.sem_inc(khi_ready, -1)
            if first:
                pool.drain()
            nc.gpsimd.tensor_tensor(kr[:, :], kf[:, :], kparts[:, 0, :], ALU.subtract).then_inc(kr_ready, 1)
            pool.wait_ge(kmid_ready, 1)
            pool.sem_inc(kmid_ready, -1)
            pool.drain()
            nc.gpsimd.tensor_tensor(kparts[:, 2, :], kr[:, :], kparts[:, 1, :], ALU.subtract).then_inc(ksplit, 1)

        def sp_body(par, exp, mx_on, prep, vals, epi, b):
            if prep:
                sp.dma_start(ctxT[:, par, :], d["ctxT"][bass.ds(b + 2, 1)].rearrange("a p k -> p (a k)"))\
                    .then_inc(ctx_in[par], 16)
                if first:
                    sp.dma_start(keep[:, :], keepscr[bass.ds(b + 2, 1), :].broadcast_to([P, S2]))\
                        .then_inc(mask_landed, 16)
                else:
                    sp.dma_start(mask_in[:, :, :], d["mask"][bass.ds(b + 2, 1)]
                                 .rearrange("a (t p) k -> p (a t) k", p=P)).then_inc(mask_landed, 16)
                sp.wait_ge(qsplit, 1)
                sp.sem_inc(qsplit, -1)
                sp.dma_start(qscr[par, 0:3].rearrange("s p c q -> (p c) s q"),
                             qparts[:].rearrange("p s j q -> p s (j q)")).then_inc(staged, 16)
                sp.wait_ge(ksplit, 1)
                sp.sem_inc(ksplit, -1)
                sp.dma_start(kscr[par].rearrange("s p c k -> (p c) s k"), kparts[:, :, :]).then_inc(staged, 16)
                sp.wait_ge(staged, 32)
                sp.sem_inc(staged, -32)
                sp.sem_inc(parts_free, 1)
            if first and not exp and prep:
                sp.wait_ge(kx_ready, b + 3)
            for half in range(2):
                if exp or mx_on:
                    sp.wait_ge(half_done, half + 1)
                if prep:
                    ps = slice(4 * half, 4 * half + 4)
                    for i in range(NPROD):
                        rows = slice(i * ROWS_OF_HEADS, (i + 1) * ROWS_OF_HEADS)
                        sp.dma_start(kx[rows, par, ps, 0:S2], kscr[par, K_PARTS[i], ps].rearrange("p c k -> c p k"))\
                            .then_inc(parts_in[half], 16)
                        sp.dma_start(qx[rows, par, ps].rearrange("c p j q -> c p (j q)"),
                                     qscr[par, Q_PARTS[i], ps].rearrange("p c q -> c p q"))\
                            .then_inc(parts_in[half], 16)
                    sp.dma_start(qx[MAX_ROW:BIAS_ROW, par, ps].rearrange("c p j q -> c p (j q)"),
                                 qscr[par, 3, ps, 0:6].rearrange("p c q -> c p q")).then_inc(parts_in[half], 16)
                    row = bass.ds(b + 2, 1) if first else slice(B, B + 1)
                    sp.dma_start(kx[BIAS_ROW:BIAS_ROW + 1, par, ps, :],
                                 bscr[row, :].unsqueeze(1).broadcast_to([1, 4, S2P]))\
                        .then_inc(parts_in[half], 16)
            if exp:
                sp.sem_inc(half_done, -2)
            elif mx_on:
                sp.wait_ge(half_done, 3)
                sp.sem_inc(half_done, -3)

        pe = act = dve = pool = sp = None

        before = [(-2, dict(exp=0, mx_on=0, prep=1, vals=0, epi=0)),
                  (-1, dict(exp=0, mx_on=1, prep=1, vals=1, epi=0))]
        steady = dict(exp=1, mx_on=1, prep=1, vals=1, epi=1)
        after = [(B - 2, dict(exp=1, mx_on=1, prep=0, vals=1, epi=1)),
                 (B - 1, dict(exp=1, mx_on=0, prep=0, vals=0, epi=1)),
                 (B, dict(exp=0, mx_on=0, prep=0, vals=0, epi=1))]

        def ones_in_keys(dve, par):
            if first:
                nc.vector.memset(kx[:, par], 1.0).then_inc(kx_ready, 1)

        def whole(eng, body, with_batch):
            def one(b, par, flags):
                if with_batch:
                    body(par, b=b, **flags)
                else:
                    body(par, **flags)
            for b, flags in before:
                one(b, b % 2, flags)
                if body is dve_body:
                    ones_in_keys(eng, b % 2)
            with eng.Fori(0, (B - 2) // 2) as i:
                for par in range(2):
                    one(i * 2 + par, par, steady)
            for b, flags in after:
                one(b, b % 2, flags)

        with nc.Block() as block:
            @block.tensor
            def _(eng):
                nonlocal pe
                pe = eng
                pe.sem_inc(probs_used, UNITS - LAG)
                whole(eng, pe_body, False)

            @block.scalar
            def _(eng):
                nonlocal act
                act = eng
                act.sem_inc(tail_ready, LAG)
                act.sem_inc(group_copied, GROUPS - 1)
                whole(eng, act_body, False)

            @block.vector
            def _(eng):
                nonlocal dve
                dve = eng
                whole(eng, dve_body, True)

            @block.gpsimd
            def _(eng):
                nonlocal pool
                pool = eng
                pool.sem_inc(mbias_free, 2)
                pool.sem_inc(step_added, 1)
                whole(eng, pool_body, True)

            @block.sync
            def _(eng):
                nonlocal sp
                sp = eng
                sp.sem_inc(parts_free, 1)
                whole(eng, sp_body, True)
                sp.drain()


def ternary_ffn(nc, x, stats, ident, d):
    FC = FF // P
    LANES = 4
    with ExitStack() as ctx:
        def sb(name, shape, dt=F32):
            return ctx.enter_context(nc.sbuf_tensor(f"f0_{name}", shape, dt))

        def sem(name):
            return ctx.enter_context(nc.semaphore(f"f0_{name}"))

        bn, mv, ve, rstd, minus_half = stats
        w = [sb("w_fc", [P, FF]), sb("w_proj", [P, FC, D])]
        flat = [w[0][:, :], w[1][:, :, :].rearrange("p c d -> p (c d)")]
        mag = sb("mag", [P, 2, FF])
        neg = sb("neg", [P, 2, FF])
        part = sb("part", [P, 2])
        gam = sb("gam", [P, 2])
        rgam = sb("rgam", [P, 2])
        ones = sb("ones", [P, P])
        lw = sb("lw", [P, FC])
        lb = sb("lb", [P, FC])
        gate = sb("gate", [P, 1])
        tgate = sb("tgate", [P, 1])
        xn = sb("xn", [P, LANES, D])
        xnT = sb("xnT", [P, LANES, P])
        h = sb("h", [P, LANES, FF])
        hn = sb("hn", [P, LANES, FF])
        hT = sb("hT", [P, LANES, FC, P])
        hbn = sb("hbn", [P, LANES, 6])
        hmv = sb("hmv", [P, LANES, 2])
        hve = sb("hve", [P, LANES])
        hrs = sb("hrs", [P, LANES])
        pa = [ctx.enter_context(nc.psum_tensor(f"f0_pa{i}", [P, 512], F32)) for i in range(LANES)]
        pb = [ctx.enter_context(nc.psum_tensor(f"f0_pb{i}", [P, 512], F32)) for i in range(LANES)]

        loaded, mag_ready, sums_ready, gam_ready = sem("loaded"), sem("mag_ready"), sem("sums_ready"), sem("gam_ready")
        ve_ready, rstd_ready = sem("ve_ready"), sem("rstd_ready")
        w_ready = sem("w_ready")
        xn_ready = sem("xn_ready")
        xnT_ready = sem("xnT_ready")
        xnT_copied = sem("xnT_copied")
        fc_ready = sem("fc_ready")
        gelu_ready = sem("gelu_ready")
        hve_ready = sem("hve_ready")
        hrs_ready = sem("hrs_ready")
        hn_ready = [sem("hn_ready0"), sem("hn_ready1")]
        hn_used = sem("hn_used")
        hT_ready = sem("hT_ready")
        hT_copied = sem("hT_copied")
        proj_ready = [sem("proj_ready0"), sem("proj_ready1")]
        proj_read = sem("proj_read")


        def pe_round(pe, n, par, fwd, proj, add):
            if fwd:
                for i in range(LANES):
                    pe.wait_ge(xn_ready, i + 1)
                    nc.tensor.transpose(pa[i][:, 0:P], xn[:, i, :], ident[:, :]).then_inc(xnT_ready, 1)
                for i in range(LANES):
                    pe.wait_ge(xnT_copied, i + 1)
                    if add:
                        pe.wait_ge(proj_read, i + 1)
                    nc.tensor.matmul(pb[i][:, :], xnT[:, i, :], w[0][:, :], start=True, stop=True)\
                        .then_inc(fc_ready, 1)
                pe.sem_inc(xn_ready, -LANES)
                pe.sem_inc(xnT_copied, -LANES)
            elif add:
                pe.wait_ge(proj_read, LANES)
            if add:
                pe.sem_inc(proj_read, -LANES)
            if proj:
                for i in range(LANES):
                    pe.wait_ge(hn_ready[1 - par], i + 1)
                    for c in range(FC):
                        mm = nc.tensor.transpose(pa[i][:, c * P:(c + 1) * P],
                                                 hn[:, i, c * P:(c + 1) * P], ident[:, :])
                    mm.then_inc(hT_ready, 1)
                    pe.drain().then_inc(hn_used, 1)
                for i in range(LANES):
                    pe.wait_ge(hT_copied, i + 1)
                    for c in range(FC):
                        mm = nc.tensor.matmul(pb[i][:, 0:D], hT[:, i, c, :], w[1][:, c, :],
                                              start=(c == 0), stop=(c == FC - 1))
                    mm.then_inc(proj_ready[1 - par], 1)
                pe.sem_inc(hn_ready[1 - par], -LANES)
                pe.sem_inc(hT_copied, -LANES)

        def act_round(act, n, par, fwd, proj, add):
            if fwd:
                for i in range(LANES):
                    act.wait_ge(xnT_ready, i + 1)
                    nc.scalar.copy(xnT[:, i, :], pa[i][:, 0:P]).then_inc(xnT_copied, 1)
                for i in range(LANES):
                    act.wait_ge(fc_ready, i + 1)
                    nc.scalar.activation(h[:, i, :], pb[i][:, :], ACT.Gelu).then_inc(gelu_ready, 1)
                act.sem_inc(xnT_ready, -LANES)
                act.sem_inc(fc_ready, -LANES)
            if proj:
                for i in range(LANES):
                    act.wait_ge(hT_ready, i + 1)
                    for c in range(FC):
                        ins = nc.scalar.activation(hT[:, i, c, :], pa[i][:, c * P:(c + 1) * P], ACT.Identity,
                                                   scale=lw[:, c:c + 1], bias=lb[:, c:c + 1])
                    ins.then_inc(hT_copied, 1)
                act.sem_inc(hT_ready, -LANES)

        def dve_round(dve, n, par, fwd, proj, add):
            def normalise(i):
                dve.wait_ge(hrs_ready, i + 1)
                if proj:
                    dve.wait_ge(hn_used, i + 1)
                nc.vector.tensor_scalar(hn[:, i, :], h[:, i, :], hmv[:, i, 0:1], hrs[:, i:i + 1],
                                        ALU.subtract, ALU.mult).then_inc(hn_ready[par], 1)

            if fwd:
                for i in range(LANES):
                    t = n * LANES + i
                    nc.vector.tensor_scalar(xn[:, i, :], x[:, bass.ds(t + QT, 1), :].rearrange("p a c -> p (a c)"),
                                            mv[:, bass.ds(t, 1), 0], rstd[:, bass.ds(t, 1)],
                                            ALU.subtract, ALU.mult).then_inc(xn_ready, 1)
            if add:
                for i in range(LANES):
                    dve.wait_ge(proj_ready[par], i + 1)
                    at = x[:, bass.ds((n - 2) * LANES + i + QT, 1), :].rearrange("p a c -> p (a c)")
                    nc.vector.scalar_tensor_tensor(out=at, in0=pb[i][:, 0:D], scalar=tgate[:, 0:1], in1=at,
                                                   op0=ALU.mult, op1=ALU.add).then_inc(proj_read, 1)
                dve.sem_inc(proj_ready[par], -LANES)
            if fwd:
                for i in range(LANES):
                    dve.wait_ge(gelu_ready, i + 1)
                    nc.vector.bn_stats(hbn[:, i, :], h[:, i, :])
                    dve.drain()
                    nc.vector.bn_aggr(hmv[:, i, :], hbn[:, i, :])
                    dve.drain()
                    nc.vector.tensor_scalar(hve[:, i:i + 1], hmv[:, i, 1:2], LN_EPS, None, ALU.add)\
                        .then_inc(hve_ready, 1)
                    if i:
                        normalise(i - 1)
                normalise(LANES - 1)
                dve.sem_inc(gelu_ready, -LANES)
                dve.sem_inc(hrs_ready, -LANES)
            elif proj:
                dve.wait_ge(hn_used, LANES)
            if proj:
                dve.sem_inc(hn_used, -LANES)

        def rounds(eng, one):
            last = NT // LANES
            one(eng, 0, 0, fwd=1, proj=0, add=0)
            one(eng, 1, 1, fwd=1, proj=1, add=0)
            with eng.Fori(0, (last - 2) // 2) as i:
                for par in range(2):
                    one(eng, i * 2 + 2 + par, par, fwd=1, proj=1, add=1)
            one(eng, last, last % 2, fwd=0, proj=1, add=1)
            one(eng, last + 1, (last + 1) % 2, fwd=0, proj=0, add=1)

        with nc.Block() as block:
            stats_dve, stats_pool = layer_norm_stats(nc, block, x, bn, mv, ve, rstd, minus_half,
                                                     ve_ready, rstd_ready)

            @block.sync
            def _(sp):
                sp.dma_start(w[0][:, :], d["w_fcT"]).then_inc(loaded, 16)
                sp.dma_start(w[1][:, :, :], d["w_projT"].rearrange("(c p) d -> p c d", p=P)).then_inc(loaded, 16)
                sp.dma_start(lw[:, :], d["ln_w"]).then_inc(loaded, 16)
                sp.dma_start(lb[:, :], d["ln_b"]).then_inc(loaded, 16)
                sp.dma_start(gate[:, :], d["gate"].partition_broadcast(P)).then_inc(loaded, 16)

            @block.tensor
            def _(pe):
                pe.wait_ge(mag_ready, 1)
                nc.tensor.matmul(pa[0][:, 0:2], ones[:, :], part[:, :], start=True, stop=True)\
                    .then_inc(sums_ready, 1)
                pe.wait_ge(w_ready, 1)
                rounds(pe, pe_round)

            @block.scalar
            def _(act):
                act.wait_ge(loaded, 80)
                nc.scalar.activation(tgate[:, :], gate[:, :], ACT.Tanh)
                rounds(act, act_round)

            @block.gpsimd
            def _(pool):
                stats_pool(pool)
                with pool.Fori(0, NT // LANES):
                    for i in range(LANES):
                        pool.wait_ge(hve_ready, i + 1)
                        nc.gpsimd.tensor_tensor(hrs[:, i:i + 1], hve[:, i:i + 1], minus_half[:, i:i + 1], ALU.pow)\
                            .then_inc(hrs_ready, 1)
                    pool.sem_inc(hve_ready, -LANES)

            @block.vector
            def _(dve):
                stats_dve(dve)
                nc.vector.memset(ones[:], 1.0)
                dve.wait_ge(loaded, 80)
                for i in range(2):
                    nc.vector.tensor_reduce(part[:, i:i + 1], flat[i], AX.X, ALU.add, apply_absolute_value=True)
                dve.drain().then_inc(mag_ready, 1)
                dve.wait_ge(sums_ready, 1)
                nc.vector.tensor_scalar(gam[:, :], pa[0][:, 0:2], 1.0 / (D * FF), GAMMA_EPS, ALU.mult, ALU.add)
                dve.drain()
                nc.vector.reciprocal(rgam[:, :], gam[:, :])
                dve.drain()
                for i in range(2):
                    nc.vector.tensor_scalar(mag[:, i, :], flat[i], rgam[:, i:i + 1], 0.5, ALU.mult, ALU.is_gt)
                    nc.vector.tensor_scalar(neg[:, i, :], flat[i], rgam[:, i:i + 1], -0.5, ALU.mult, ALU.is_lt)
                dve.drain()
                for i in range(2):
                    nc.vector.tensor_tensor(flat[i], mag[:, i, :], neg[:, i, :], ALU.subtract)
                dve.drain().then_inc(w_ready, 1)
                dve.wait_ge(rstd_ready, 1)
                rounds(dve, dve_round)


def expert_ffn(nc, x, stats, ident, d, out):
    TT = 4
    T = TT * P
    NG = NT // TT
    FC = FE // P
    with ExitStack() as ctx:
        def sb(name, shape, dt=F32):
            return ctx.enter_context(nc.sbuf_tensor(f"f1_{name}", shape, dt))

        def pb(name):
            return ctx.enter_context(nc.psum_tensor(f"f1_{name}", [P, 512], F32))

        def sem(name):
            return ctx.enter_context(nc.semaphore(f"f1_{name}"))

        bn, mv, ve, rstd, minus_half = stats
        w1 = sb("w1", [P, NE, FE])
        w3 = sb("w3", [P, NE, FE])
        w2 = sb("w2", [P, NE, FC, D])
        router = sb("router", [P, NE])
        below = sb("below", [P, NE, NE])
        gate = sb("gate", [P, 1])
        tgate = sb("tgate", [P, 1])
        xn = sb("xn", [P, TT, D])
        xnT = sb("xnT", [P, 2, T])
        logits = sb("logits", [P, TT, NE])
        gt = sb("gt", [P, TT, NE, NE])
        eq = sb("eq", [P, TT, NE, NE])
        rank = sb("rank", [P, TT, NE])
        sel = sb("sel", [P, TT, NE])
        picked = sb("picked", [P, TT, NE])
        both = sb("both", [P, TT])
        lead = sb("lead", [P, TT, NE])
        th = sb("th", [P, 2, TT, NE])
        comb = sb("comb", [P, TT, NE])
        sg = sb("sg", [P, 2, T])
        hT = sb("hT", [P, 4, T])
        acc = sb("acc", [P, TT, D])
        res = sb("res", [P, 2, TT, D])
        pt = pb("pt")
        pg = [pb("pg0"), pb("pg1")]
        pu = [pb("pu0"), pb("pu1")]
        po = [pb("po0"), pb("po1")]

        loaded = sem("loaded")
        ve_ready, rstd_ready = sem("ve_ready"), sem("rstd_ready")
        xn_ready = sem("xn_ready")
        xnT_ready = sem("xnT_ready")
        xnT_copied = sem("xnT_copied")
        logits_ready = sem("logits_ready")
        lead_ready = sem("lead_ready")
        th_ready = sem("th_ready")
        gates_ready = sem("gates_ready")
        ups_ready = sem("ups_ready")
        silu_ready = sem("silu_ready")
        hidden_ready = sem("hidden_ready")
        expert_ready = sem("expert_ready")
        expert_read = sem("expert_read")
        res_ready = sem("res_ready")
        stored = [sem("stored0"), sem("stored1")]
        res_free = sem("res_free")
        sg_used = sem("sg_used")
        NC = NE * FC
        AT_NEXT = 4

        def steps(eng, one):
            with eng.Fori(0, (NG - 2) // 2) as i:
                for par in range(2):
                    one(eng, i * 2 + par, par, 1)
            one(eng, NG - 2, 0, 1)
            one(eng, NG - 1, 1, 0)

        with nc.Block() as block:
            stats_dve, stats_pool = layer_norm_stats(nc, block, x, bn, mv, ve, rstd, minus_half,
                                                     ve_ready, rstd_ready)

            @block.sync
            def _(sp):
                sp.dma_start(router[:, :], d["router"]).then_inc(loaded, 16)
                sp.dma_start(below[:, :, :], d["below"].partition_broadcast(P)).then_inc(loaded, 16)
                sp.dma_start(gate[:, :], d["gate"].partition_broadcast(P)).then_inc(loaded, 16)
                sp.dma_start(w1[:, :, :], d["w1"].rearrange("e h f -> h e f")).then_inc(loaded, 16)
                sp.dma_start(w3[:, :, :], d["w3"].rearrange("e h f -> h e f")).then_inc(loaded, 16)
                sp.dma_start(w2[:, :, :, :], d["w2"].rearrange("e (c p) h -> p e c h", p=P)).then_inc(loaded, 16)
                out_v = out.rearrange("b (t p) c -> p (b t) c", p=P)
                with sp.Fori(0, NG // 2) as n:
                    for k in range(2):
                        sp.wait_ge(res_ready, k + 1)
                        sp.dma_start(out_v[:, bass.ds((n * 2 + k) * TT, TT), :], res[:, k]).then_inc(stored[k], 16)
                    for k in range(2):
                        sp.wait_ge(stored[k], 16)
                        sp.sem_inc(stored[k], -16)
                        sp.sem_inc(res_free, 1)
                    sp.sem_inc(res_ready, -2)

            def pe_next_tokens(pe, par):
                pe.wait_ge(xn_ready, 1)
                pe.sem_inc(xn_ready, -1)
                for i in range(TT):
                    mm = nc.tensor.transpose(pt[:, i * P:(i + 1) * P], xn[:, i, :], ident[:, :])
                mm.then_inc(xnT_ready, 1)

            def pe_next_logits(pe, par):
                pe.wait_ge(xnT_copied, 1)
                pe.sem_inc(xnT_copied, -1)
                for i in range(TT):
                    mm = nc.tensor.matmul(pt[:, i * NE:(i + 1) * NE], xnT[:, par, i * P:(i + 1) * P], router[:, :],
                                          start=True, stop=True)
                mm.then_inc(logits_ready, 1)

            def pe_step(pe, n, par, nxt):
                for e in range(NE + 1):
                    for c in range(FC if e < NE else 0):
                        k = e * FC + c
                        if nxt and k == AT_NEXT:
                            pe_next_tokens(pe, 1 - par)
                        if nxt and k == AT_NEXT + 2:
                            pe_next_logits(pe, 1 - par)
                        if k >= 2:
                            pe.wait_ge(hidden_ready, k - 1)
                        nc.tensor.matmul(pg[k % 2][:, :], w1[:, e, c * P:(c + 1) * P], xnT[:, par, :],
                                         start=True, stop=True).then_inc(gates_ready, 1)
                        nc.tensor.matmul(pu[k % 2][:, :], w3[:, e, c * P:(c + 1) * P], xnT[:, par, :],
                                         start=True, stop=True).then_inc(ups_ready, 1)
                    if e > 0:
                        f = e - 1
                        pe.wait_ge(hidden_ready, FC * (f + 1))
                        if f >= 2:
                            pe.wait_ge(expert_read, f - 1)
                        for i in range(TT):
                            for c in range(FC):
                                mm = nc.tensor.matmul(po[f % 2][:, i * P:(i + 1) * P],
                                                      hT[:, (f * FC + c) % 4, i * P:(i + 1) * P],
                                                      w2[:, f, c, :], start=(c == 0), stop=(c == FC - 1))
                        mm.then_inc(expert_ready, 1)
                pe.wait_ge(expert_read, NE)
                pe.sem_inc(hidden_ready, -NC)
                pe.sem_inc(expert_read, -NE)

            @block.tensor
            def _(pe):
                pe.wait_ge(loaded, 96)
                pe_next_tokens(pe, 0)
                pe_next_logits(pe, 0)
                steps(pe, pe_step)

            def act_next_tokens(act, par):
                act.wait_ge(xnT_ready, 1)
                act.sem_inc(xnT_ready, -1)
                nc.scalar.copy(xnT[:, par, :], pt[:, :]).then_inc(xnT_copied, 1)

            def act_next_weights(act, par):
                act.wait_ge(lead_ready, 1)
                act.sem_inc(lead_ready, -1)
                nc.scalar.activation(th[:, par], lead[:, :, :], ACT.Tanh, scale=0.5).then_inc(th_ready, 1)

            def act_step(act, n, par, nxt):
                for k in range(NC):
                    act.wait_ge(gates_ready, k + 1)
                    if k >= 2:
                        act.wait_ge(sg_used, k - 1)
                    nc.scalar.activation(sg[:, k % 2, :], pg[k % 2][:, :], ACT.Silu).then_inc(silu_ready, 1)
                    if nxt and k == AT_NEXT - 1:
                        act_next_tokens(act, 1 - par)
                act.wait_ge(sg_used, NC)
                act.sem_inc(gates_ready, -NC)
                act.sem_inc(sg_used, -NC)
                if nxt:
                    act_next_weights(act, 1 - par)

            @block.scalar
            def _(act):
                act.wait_ge(loaded, 96)
                nc.scalar.activation(tgate[:, :], gate[:, :], ACT.Tanh)
                act_next_tokens(act, 0)
                act_next_weights(act, 0)
                steps(act, act_step)

            @block.gpsimd
            def _(pool):
                stats_pool(pool)

            def dve_next_tokens(dve, n):
                for i in range(TT):
                    t = n * TT + i
                    ins = nc.vector.tensor_scalar(xn[:, i, :], x[:, bass.ds(t + QT, 1), :].rearrange("p a c -> p (a c)"),
                                                  mv[:, bass.ds(t, 1), 0], rstd[:, bass.ds(t, 1)],
                                                  ALU.subtract, ALU.mult)
                ins.then_inc(xn_ready, 1)

            def dve_next_experts(dve):
                dve.wait_ge(logits_ready, 1)
                dve.sem_inc(logits_ready, -1)
                nc.vector.tensor_copy(logits[:, :, :], pt[:, 0:TT * NE].rearrange("p (t e) -> p t e", e=NE))
                dve.drain()
                mine = logits[:, :, :].unsqueeze(3).broadcast_to([P, TT, NE, NE])
                other = logits[:, :, :].unsqueeze(2).broadcast_to([P, TT, NE, NE])
                nc.vector.tensor_tensor(gt[:], other, mine, ALU.is_gt)
                nc.vector.tensor_tensor(eq[:], other, mine, ALU.is_equal)
                dve.drain()
                nc.vector.tensor_tensor(eq[:], eq[:], below[:, :, :].unsqueeze(1).broadcast_to([P, TT, NE, NE]), ALU.mult)
                dve.drain()
                nc.vector.tensor_tensor(gt[:], gt[:], eq[:], ALU.add)
                dve.drain()
                nc.vector.tensor_reduce(rank[:], gt[:], AX.X, ALU.add)
                dve.drain()
                nc.vector.tensor_scalar(sel[:], rank[:], 2.0, None, ALU.is_lt)
                dve.drain()
                nc.vector.tensor_tensor(picked[:], sel[:], logits[:], ALU.mult)
                dve.drain()
                nc.vector.tensor_reduce(both[:], picked[:], AX.X, ALU.add)
                dve.drain()
                nc.vector.scalar_tensor_tensor(out=lead[:], in0=logits[:], scalar=2.0,
                                               in1=both[:, :].unsqueeze(2).broadcast_to([P, TT, NE]),
                                               op0=ALU.mult, op1=ALU.subtract).then_inc(lead_ready, 1)

            def dve_step(dve, n, par, nxt):
                if nxt:
                    dve_next_tokens(dve, n + 1)
                for e in range(NE + 1):
                    for c in range(FC if e < NE else 0):
                        k = e * FC + c
                        dve.wait_ge(silu_ready, k + 1)
                        dve.wait_ge(ups_ready, k + 1)
                        if k == 2:
                            dve.wait_ge(th_ready, 1)
                            dve.sem_inc(th_ready, -1)
                            nc.vector.tensor_scalar(th[:, par], th[:, par], 0.5, 0.5, ALU.mult, ALU.add)
                            dve.drain()
                            nc.vector.tensor_tensor(comb[:], th[:, par], sel[:], ALU.mult)
                            dve.drain()
                        nc.vector.tensor_tensor(hT[:, k % 4, :], pu[k % 2][:, :], sg[:, k % 2, :], ALU.mult)\
                            .then_inc(hidden_ready, 1)
                        dve.drain().then_inc(sg_used, 1)
                        if nxt and k == AT_NEXT + 4:
                            dve_next_experts(dve)
                    if e > 0:
                        f = e - 1
                        dve.wait_ge(expert_ready, f + 1)
                        for i in range(TT):
                            src, dst, wt = po[f % 2][:, i * P:(i + 1) * P], acc[:, i, :], comb[:, i, f:f + 1]
                            if f == 0:
                                ins = nc.vector.tensor_scalar(dst, src, wt, None, ALU.mult)
                            else:
                                ins = nc.vector.scalar_tensor_tensor(out=dst, in0=src, scalar=wt, in1=dst,
                                                                     op0=ALU.mult, op1=ALU.add)
                        ins.then_inc(expert_read, 1)
                        dve.drain()
                dve.wait_ge(res_free, par + 1)
                nc.vector.scalar_tensor_tensor(out=res[:, par], in0=acc[:], scalar=tgate[:, 0:1],
                                               in1=x[:, bass.ds(n * TT + QT, TT), :], op0=ALU.mult, op1=ALU.add)\
                    .then_inc(res_ready, 1)
                dve.sem_inc(silu_ready, -NC)
                dve.sem_inc(ups_ready, -NC)
                dve.sem_inc(expert_ready, -NE)
                if par:
                    dve.sem_inc(res_free, -2)

            @block.vector
            def _(dve):
                stats_dve(dve)
                dve.wait_ge(loaded, 96)
                dve.wait_ge(rstd_ready, 1)
                dve.sem_inc(res_free, 2)
                dve_next_tokens(dve, 0)
                dve_next_experts(dve)
                steps(dve, dve_step)


def flamingo(nc, d, out):
    with ExitStack() as ctx:
        def sb(name, shape, dt=F32):
            return ctx.enter_context(nc.sbuf_tensor(name, shape, dt))

        x = sb("x", [P, NT + QT, D])
        stats = (sb("bn", [P, NT, 6]), sb("mv", [P, NT, 2]), sb("ve", [P, NT]), sb("rstd", [P, NT]),
                 sb("minus_half", [P, NT]))
        ident = sb("ident", [P, P])
        ident_bf = sb("ident_bf", [P, P], BF16)
        head_of = sb("head_of", [P, 2])
        row_of = sb("row_of", [6, 2])
        kscr = nc.dram_tensor("key_parts", [2, 3, HP, 2 * DH, S2], BF16, kind="Internal").ap()
        qscr = nc.dram_tensor("query_parts", [2, 4, HP, 2 * DH, 2 * S], BF16, kind="Internal").ap()
        bscr = nc.dram_tensor("key_bias", [B + 1, S2P], BF16, kind="Internal").ap()
        keepscr = nc.dram_tensor("key_mask", [B, S2], BF16, kind="Internal").ap()
        consts_in = ctx.enter_context(nc.semaphore("consts_in"))

        with nc.Block() as block:
            @block.sync
            def _(sp):
                sp.dma_start(ident[:, :], d["ident"]).then_inc(consts_in, 16)
                sp.dma_start(head_of[:, :], d["head_of"]).then_inc(consts_in, 16)
                sp.dma_start(row_of[:, :], d["row_of"]).then_inc(consts_in, 16)
                sp.wait_ge(consts_in, 48)

            @block.vector
            def _(dve):
                nc.vector.memset(x[:, 0:QT, :], 0.0)
                dve.wait_ge(consts_in, 48)
                nc.vector.tensor_copy(ident_bf[:, :], ident[:, :])

        scratch = (kscr, qscr, bscr, keepscr)
        with ExitStack() as both:
            def keep(name, shape, dt):
                return both.enter_context(nc.sbuf_tensor(name, shape, dt))
            kept = (keep("kx", [P, 2, HP, S2P], BF16),
                    keep("qx", [P, 2, HP, 2, S], BF16),
                    keep("vx", [P, 2, KT, H, DH + 1], F32),
                    keep("probs", [P, NPB, 2 * S], F32),
                    keep("outT", [P, GROUPS, S], F32))
            attention(nc, 0, x, stats, ident, ident_bf, head_of, row_of, {
                "x": d["x"], "keep": d["keep"], "ctxT": d["ctxT"], "gate": d["g_xattn"][0:1],
                "wq": d["wq0"], "wk": d["wk0"], "wv": d["wv0"], "wo": d["wo0"],
                "bq": d["bq0"], "bk": d["bk0"], "bv": d["bv0"], "bo": d["bo0"]}, scratch, kept)
            ternary_ffn(nc, x, stats, ident, {
                "w_fcT": d["w_fcT"], "w_projT": d["w_projT"], "ln_w": d["ln_w"], "ln_b": d["ln_b"],
                "gate": d["g_ffn"][0:1]})
            attention(nc, 1, x, stats, ident, ident_bf, head_of, row_of, {
                "mask": d["mask"], "ctxT": d["ctxT"], "gate": d["g_xattn"][1:2],
                "wq": d["wq1"], "wk": d["wk1"], "wv": d["wv1"], "wo": d["wo1"], "bo": d["bo1"]}, scratch, kept)
        expert_ffn(nc, x, stats, ident, {
            "router": d["router"], "below": d["below"], "w1": d["w1"], "w3": d["w3"], "w2": d["w2"],
            "gate": d["g_ffn"][1:2]}, out)


def kernel(**inputs):
    import numpy as np
    import concourse.bacc as bacc
    from concourse.bass_utils import run_bass_kernel_spmd

    a = {k: np.asarray(v) for k, v in inputs.items()}
    rows = np.arange(P)
    layout = {
        "x": a["x"],
        "ctxT": a["ctx_1024"].transpose(0, 2, 1),
        "keep": a["mask_BxS2_bf1"].view(np.uint8),
        "mask": a["mask_Bx1xSxS2_ik1"][:, 0],
        "g_xattn": a["g_xattn"], "g_ffn": a["g_ffn"],
        "wq0": a["L0_xattn_Wq"].T, "wk0": a["L0_xattn_Wk"].T, "wv0": a["L0_xattn_Wv"].T, "wo0": a["L0_xattn_Wo"].T,
        "bq0": a["L0_xattn_bq"].reshape(P, 1), "bk0": a["L0_xattn_bk"].reshape(P, 1),
        "bv0": a["L0_xattn_bv"], "bo0": a["L0_xattn_bo"],
        "w_fcT": a["L0_ffn_W_fc"].T, "w_projT": a["L0_ffn_W_proj"].T,
        "ln_w": a["L0_ffn_ln_w"].reshape(FF // P, P).T, "ln_b": a["L0_ffn_ln_b"].reshape(FF // P, P).T,
        "wq1": a["L1_xattn_Wq"].T, "wk1": a["L1_xattn_Wk"].T, "wv1": a["L1_xattn_Wv"].T, "wo1": a["L1_xattn_Wo"].T,
        "bo1": a["L1_xattn_bo"],
        "router": a["L1_ffn_router_w"], "w1": a["L1_ffn_w1"], "w3": a["L1_ffn_w3"], "w2": a["L1_ffn_w2"],
        "ident": np.eye(P, dtype=np.float32),
        "head_of": (rows[:, None] // DH % 2 == np.arange(2)).astype(np.float32),
        "row_of": (np.arange(6)[:, None] // 3 == np.arange(2)).astype(np.float32),
        "below": np.tril(np.ones((NE, NE), np.float32), -1),
    }
    nc = bacc.Bacc("TRN2", target_bir_lowering=False, num_devices=1)
    arrays, d = {}, {}
    for name, v in layout.items():
        v = np.ascontiguousarray(v)
        arrays[f"in_{name}"] = v
        d[name] = nc.dram_tensor(f"in_{name}", v.shape, mybir.dt.from_np(v.dtype), kind="ExternalInput").ap()
    out = nc.dram_tensor("out_x", (B, S, D), F32, kind="ExternalOutput").ap()
    flamingo(nc, d, out)
    r = run_bass_kernel_spmd(nc, [arrays], core_ids=[0])
    return r.results[0]["out_x"]
```
